# Optimizing a Trainium2 kernel written in Bass

```python
import numpy as np
import jax
import jax.numpy as jnp

def _softmax(x, axis=-1):
    return jax.nn.softmax(x, axis=axis)

def _gelu(x):
    return jax.nn.gelu(x, approximate=True)

def _silu(x):
    return jax.nn.silu(x)

def _sigmoid(x):
    return jax.nn.sigmoid(x)

def _layernorm(x, axis=-1, eps=1e-05):
    m = jnp.mean(x, axis=axis, keepdims=True)
    v = jnp.var(x, axis=axis, keepdims=True)
    return (x - m) / jnp.sqrt(v + eps)

def _scatter_add(tgt, idx, src, axis=0):
    return tgt.at[idx].add(src)

def _segment_sum(src, seg, n):
    return jax.ops.segment_sum(src, seg, n)
kernel_name = 'mk_adj_resnorm_d4_adj_r2_9172c1'

def setup_inputs(seed: int=0):
    np.random.seed(seed)
    _w = jnp.asarray

    def _rec_inputs():
        import jax
        import jax.numpy as jnp
        _gk = jax.random.key(seed)
        x = -0.000929 + 1 * jax.random.normal(jax.random.fold_in(_gk, 1), (4096, 128), jnp.float32)
        _w = (1.0 + jnp.arange(4096, dtype=jnp.float32)) ** (-0.5)
        _w = _w / _w.mean()
        _pij = jnp.clip(0.00390625 * _w[:, None] * _w[None, :], 0.0, 1.0)
        _a = jax.random.uniform(jax.random.fold_in(_gk, 2), (4096, 4096)) < _pij
        _a = jnp.logical_or(_a, jnp.eye(4096, dtype=bool))
        _af = _a.astype(jnp.float32)
        _af = _af * jax.random.uniform(jax.random.fold_in(_gk, 3), (4096, 4096), jnp.float32, 0.05, 1)
        adj = _af
        return (x, adj)
    x, adj = _rec_inputs()

    def _L0_gnn_setup():
        import jax, jax.numpy as jnp
        import numpy as np
        N = 4096
        F_IN = 128
        F_OUT = 128
        key = jax.random.key(seed)
        k1, k2, k3, k4, k5 = jax.random.split(key, 5)
        x = jax.random.normal(k1, (N, F_IN), dtype=jnp.float32)
        adj = jax.random.uniform(k2, (N, N), dtype=jnp.float32)
        kernel = jax.random.normal(k3, (F_IN, F_OUT), dtype=jnp.float32) * 0.05
        bias = jax.random.normal(k4, (F_OUT,), dtype=jnp.float32) * 0.05
        beta = jax.random.uniform(k5, (N,), dtype=jnp.float32)
        return {'x': x, 'adj': adj, 'kernel': kernel, 'bias': bias, 'beta': beta}
    _L0_gnn_all = _L0_gnn_setup()
    _L0_gnn_in = {k: v for k, v in _L0_gnn_all.items() if k in ('kernel', 'bias', 'beta')}
    del _L0_gnn_all

    def _L1_gnn_setup():
        import jax, jax.numpy as jnp
        import numpy as np
        N, D_IN, F1, F2, D_OUT = (5000, 128, 20, 20, 128)

        def _gcn(h, adj, W, b):
            return adj @ (h @ W) + b
        key = jax.random.key(seed)
        ks = jax.random.split(key, 8)
        x = jax.random.normal(ks[0], (N, D_IN), dtype=jnp.float32)
        adj = jax.random.uniform(ks[1], (N, N), dtype=jnp.float32)

        def glorot(k, fi, fo):
            s = 1.0 / np.sqrt(fi)
            return jax.random.uniform(k, (fi, fo), dtype=jnp.float32, minval=-s, maxval=s)
        W1 = glorot(ks[2], D_IN, F1)
        b1 = jnp.zeros((F1,), jnp.float32)
        W2 = glorot(ks[3], F1, F2)
        b2 = jnp.zeros((F2,), jnp.float32)
        W3 = glorot(ks[4], F2, D_OUT)
        b3 = jnp.zeros((D_OUT,), jnp.float32)
        return {'x': x, 'adj': adj, 'W1': W1, 'b1': b1, 'W2': W2, 'b2': b2, 'W3': W3, 'b3': b3}
    _L1_gnn_all = _L1_gnn_setup()
    _L1_gnn_in = {k: v for k, v in _L1_gnn_all.items() if k in ('W1', 'b1', 'W2', 'b2', 'W3', 'b3')}
    del _L1_gnn_all

    def _L2_gnn_setup():
        import jax, jax.numpy as jnp
        import numpy as np
        OVERFLOW_MARGIN = 1e-08
        N, D, OUT = (4096, 128, 128)
        key = jax.random.key(seed)
        k1, k2, k3 = jax.random.split(key, 3)
        values = jax.random.normal(k1, (N, D), dtype=jnp.float32)
        adjacency = jax.random.uniform(k2, (N, N), dtype=jnp.float32)
        W = jax.random.normal(k3, (D, OUT), dtype=jnp.float32) * 0.05
        b = jnp.zeros((OUT,), dtype=jnp.float32)
        return {'values': values, 'adjacency': adjacency, 'W': W, 'b': b}
    _L2_gnn_all = _L2_gnn_setup()
    _L2_gnn_in = {k: v for k, v in _L2_gnn_all.items() if k in ('W', 'b')}
    del _L2_gnn_all

    def _L3_gnn_setup():
        import jax, jax.numpy as jnp
        import numpy as np
        N = 4096
        D = 128

        def _xavier(key, shape):
            fan_in, fan_out = shape
            limit = float(np.sqrt(6.0 / (fan_in + fan_out)))
            return jax.random.uniform(key, shape, jnp.float32, -limit, limit)
        key = jax.random.key(seed)
        kH, kA, k1, k2, k3, k4 = jax.random.split(key, 6)
        return {'H': jax.random.normal(kH, (N, D), jnp.float32), 'adj': jax.random.uniform(kA, (N, N), jnp.float32), 'W_l': _xavier(k1, (D, D)), 'W_r': _xavier(k2, (D, D)), 'W_h': _xavier(k3, (D, D)), 'W_g': _xavier(k4, (D, D)), 'gamma': jnp.zeros((1,), jnp.float32)}
    _L3_gnn_all = _L3_gnn_setup()
    _L3_gnn_in = {k: v for k, v in _L3_gnn_all.items() if k in ('W_l', 'W_r', 'W_h', 'W_g', 'gamma')}
    del _L3_gnn_all
    return {'x': x, 'adj': adj, 'L0_gnn_kernel': _L0_gnn_in['kernel'], 'L0_gnn_bias': _L0_gnn_in['bias'], 'L0_gnn_beta': _L0_gnn_in['beta'], 'L1_gnn_W1': _L1_gnn_in['W1'], 'L1_gnn_b1': _L1_gnn_in['b1'], 'L1_gnn_W2': _L1_gnn_in['W2'], 'L1_gnn_b2': _L1_gnn_in['b2'], 'L1_gnn_W3': _L1_gnn_in['W3'], 'L1_gnn_b3': _L1_gnn_in['b3'], 'L2_gnn_W': _L2_gnn_in['W'], 'L2_gnn_b': _L2_gnn_in['b'], 'L3_gnn_W_l': _L3_gnn_in['W_l'], 'L3_gnn_W_r': _L3_gnn_in['W_r'], 'L3_gnn_W_h': _L3_gnn_in['W_h'], 'L3_gnn_W_g': _L3_gnn_in['W_g'], 'L3_gnn_gamma': _L3_gnn_in['gamma']}

def reference(x, adj, L0_gnn_kernel, L0_gnn_bias, L0_gnn_beta, L1_gnn_W1, L1_gnn_b1, L1_gnn_W2, L1_gnn_b2, L1_gnn_W3, L1_gnn_b3, L2_gnn_W, L2_gnn_b, L3_gnn_W_l, L3_gnn_W_r, L3_gnn_W_h, L3_gnn_W_g, L3_gnn_gamma):
    import jax
    import jax.numpy as jnp

    def _L0_gnn_ref(x, adj, kernel, bias, beta):
        import jax, jax.numpy as jnp
        import numpy as np
        N = 4096
        F_IN = 128
        F_OUT = 128
        inv_deg = 1.0 / (jnp.sum(adj, axis=1) + beta)
        agg = adj @ x + beta[:, None] * x
        out = inv_deg[:, None] * agg @ kernel + bias
        return out

    def _L1_gnn_ref(x, adj, W1, b1, W2, b2, W3, b3):
        import jax, jax.numpy as jnp
        import numpy as np
        N, D_IN, F1, F2, D_OUT = (5000, 128, 20, 20, 128)

        def _gcn(h, adj, W, b):
            return adj @ (h @ W) + b
        h = jax.nn.relu(_gcn(x, adj, W1, b1))
        h = jax.nn.relu(_gcn(h, adj, W2, b2))
        h = jax.nn.relu(_gcn(h, adj, W3, b3))
        return jax.nn.relu(h + x)

    def _L2_gnn_ref(values, adjacency, W, b):
        import jax, jax.numpy as jnp
        import numpy as np
        OVERFLOW_MARGIN = 1e-08
        N, D, OUT = (4096, 128, 128)
        fc_sc = values @ W + b
        d = jnp.sum(adjacency, axis=1)
        d_inv_sqrt = 1.0 / (jnp.sqrt(d) + OVERFLOW_MARGIN)
        laplacian = adjacency * d_inv_sqrt[:, None] * d_inv_sqrt[None, :]
        return laplacian @ fc_sc

    def _L3_gnn_ref(H, adj, W_l, W_r, W_h, W_g, gamma):
        import jax, jax.numpy as jnp
        import numpy as np
        N = 4096
        D = 128

        def _xavier(key, shape):
            fan_in, fan_out = shape
            limit = float(np.sqrt(6.0 / (fan_in + fan_out)))
            return jax.random.uniform(key, shape, jnp.float32, -limit, limit)
        H_l = H @ W_l
        H_r = H @ W_r
        S = H_l @ H_r.T
        beta = jax.nn.softmax(S, axis=-1)
        B = beta @ H
        O = B @ W_h @ W_g
        return adj @ H + gamma * O
    x = _layernorm(x + _L0_gnn_ref(x, adj, L0_gnn_kernel, L0_gnn_bias, L0_gnn_beta), axis=-1)
    x = _layernorm(x + _L1_gnn_ref(x, adj, L1_gnn_W1, L1_gnn_b1, L1_gnn_W2, L1_gnn_b2, L1_gnn_W3, L1_gnn_b3), axis=-1)
    x = _layernorm(x + _L2_gnn_ref(x, adj, L2_gnn_W, L2_gnn_b), axis=-1)
    x = _layernorm(x + _L3_gnn_ref(x, adj, L3_gnn_W_l, L3_gnn_W_r, L3_gnn_W_h, L3_gnn_W_g, L3_gnn_gamma), axis=-1)
    return x

_drawn_inputs = setup_inputs


def setup_inputs(seed=0):
    import zlib

    import numpy as np

    out = dict(_drawn_inputs(seed))
    spreads = {'L1_gnn_b1': (0.0, 0.1),
     'L1_gnn_b2': (0.0, 0.8),
     'L1_gnn_b3': (0.0, 0.8),
     'L2_gnn_b': (0.0, 0.1)}
    factors = {'L0_gnn_beta': 8.0}
    for name, (base, spread) in spreads.items():
        noise = np.random.default_rng([zlib.crc32(name.encode()), seed]).standard_normal(out[name].shape)
        drawn = base * np.exp(spread * noise) if base else spread * noise
        out[name] = jnp.asarray(drawn.astype(out[name].dtype))
    for name, factor in factors.items():
        out[name] = (out[name] * factor).astype(out[name].dtype)
    return out
```

```python
from contextlib import ExitStack

import numpy as np

import concourse.bass as bass
from concourse import mybir

F32 = mybir.dt.float32
F32R = mybir.dt.float32r
ALU = mybir.AluOpType
ACT = mybir.ActivationFunctionType
AX_X = mybir.AxisListType.X

P = 128
N = 4096
D = 128
H = 20
NB = N // P
CB = 4
CW = CB * P
NC = NB // CB
GB = 4
NG = NB // GB
NS = NG - 1
TW = GB * CW
NSWEEP = 6
NARROW = (1, 2, 3)
RAW = 4
EPS = 1e-5
SQRT_GUARD = 1e-8
QB = 2
QW = QB * P
NQ = NB // QB
NSTEP = NB // 2
EQ = 4
EW = N // EQ

STAGES = {
    "xb": (0, 3, 4, 5), "bx": (0,), "xw": (0, 3, 4), "at": range(6), "rs": (0,), "sq": (0,),
    "h1": (1, 2), "dinv0": (0,), "deg": (0,), "inv": (0,), "dg2": (0,), "t1": (0, 3, 4), "t2": (3,),
    "resid": (0, 3, 4), "bst": (0, 3, 4), "agg": (0, 3, 4), "var": (0, 3, 4), "std": (0, 3, 4),
    "rc": (0, 3, 4), "rstd": (0, 3, 4), "norm": (0, 3, 4), "xt": (0, 3), "ht": (5,), "uw": (0, 1, 2),
    "vt": (3,), "vw": (3,), "xfin": (5,), "mm1": range(6), "mm2": (1, 2), "tx": (0, 3), "mu": (0, 3),
}


def done(stage, s, c):
    return c + (1 + NC * sum(q < s for q in STAGES[stage]))


def build(nc, adj_t, x_in, beta_in, ident_in, comb_in, w, out):
    with ExitStack() as ctx:
        def sb(name, shape, dt=F32, on=ctx):
            return on.enter_context(nc.sbuf_tensor(name, shape, dt))

        def bank(name):
            return ctx.enter_context(nc.psum_tensor(name, [P, CW], F32))

        ident = sb("ident", [P, P])
        comb = sb("comb", [2 * H, P])
        ones_f = sb("ones_f", [P, P])
        ones_r = sb("ones_r", [P, P], F32R)
        k0 = sb("k0", [P, D])
        w1 = sb("w1", [P, H])
        w2 = sb("w2", [H, H])
        w3 = sb("w3", [2 * H, D])
        w_l2 = sb("w_l2", [P, D])
        w_q, w_k, w_h, w_g = (sb(n, [P, D]) for n in ("w_q", "w_k", "w_h", "w_g"))
        bias0, bias3, bias_l2 = (sb(n, [P, D]) for n in ("bias0", "bias3", "bias_l2"))
        b1, b2 = sb("b1", [H, 1]), sb("b2", [H, 1])
        gamma = sb("gamma", [P, 1])
        beta = sb("beta", [P, NB])
        dinv = sb("dinv", [P, NB])
        rs_row = sb("rs_row", [1, CW])
        sq, deg, inv, dg2 = (sb(n, [P, CB]) for n in ("sq", "deg", "inv", "dg2"))
        stats = sb("stats", [P, CB, 6])
        mv = sb("mv", [P, CB, 2])
        ve, std, rstd, nmr = (sb(n, [P, CB]) for n in ("ve", "std", "rstd", "nmr"))
        mv_all = sb("mv_all", [P, NB * 2])

        x = sb("x", [P, NB * D])
        v = sb("v", [P, NB * D])
        st_hi = sb("st_hi", [P, NB * D], F32R)
        st_lo = sb("st_lo", [P, NB * D], F32R)

        with ExitStack() as swp:
            resident = sb("resident", [P, NC * TW], F32, swp)
            raw = sb("raw", [P, RAW, TW], F32, swp)
            t_hi = sb("t_hi", [P, 2, TW], F32R, swp)
            t_lo = sb("t_lo", [P, 2, TW], F32R, swp)
            at = sb("at", [P, CW], F32, swp)
            xt = sb("xt", [P, CW], F32, swp)
            xb = sb("xb", [P, CW], F32, swp)
            xs = sb("xs", [P, CW], F32, swp)
            xn = sb("xn", [P, CW], F32, swp)
            bx = sb("bx", [P, CW], F32, swp)

        with ExitStack() as att:
            pb = [sb(f"pb{i}", [P, QB, N], F32, att) for i in range(2)]
            k_hi = sb("k_hi", [P, N], F32R, att)
            k_lo = sb("k_lo", [P, N], F32R, att)
            q_hi = sb("q_hi", [P, QW], F32R, att)
            q_lo = sb("q_lo", [P, QW], F32R, att)
            p_hi = sb("p_hi", [P, 2, 2 * QW], F32R, att)
            p_lo = sb("p_lo", [P, 2, 2 * QW], F32R, att)
            bt = sb("bt", [P, QW], F32, att)
            ct = sb("ct", [P, QW], F32, att)
            o_s = sb("o_s", [P, QW], F32, att)
            mx = [sb(f"mx{i}", [P, QB * NC], F32, att) for i in range(2)]
            mxr = sb("mxr", [P, QB], F32, att)
            nm = [sb(f"nm{i}", [P, QB], F32, att) for i in range(2)]
            ls = [sb(f"ls{i}", [P, QB * EQ], F32, att) for i in range(2)]
            lsum, lrec, lg = (sb(n, [P, QB], F32, att) for n in ("lsum", "lrec", "lg"))
            stats_a = sb("stats_a", [P, QB, 6], F32, att)
            mv_a = sb("mv_a", [P, QB, 2], F32, att)
            ve_a, std_a, rstd_a, nmr_a = (sb(n, [P, NB], F32, att) for n in ("ve_a", "std_a", "rstd_a", "nmr_a"))

        acc = [bank("acc0"), bank("acc1")]
        rs = [bank("rs0"), bank("rs1")]
        e0, e1, e2, e3 = (bank(f"e{i}") for i in range(4))

        def sem(name):
            return ctx.enter_context(nc.semaphore(name))

        past_wait = sem("past_wait")
        const_in, memset_done, out_done = sem("const_in"), sem("memset_done"), sem("out_done")
        x_in0, x_in1 = sem("x_in0"), sem("x_in1")
        raw_in = [sem(f"raw_in{i}") for i in range(RAW)]
        res_in = sem("res_in")
        hi_done, lo_done, pe_tile, pe_acc = sem("hi_done"), sem("lo_done"), sem("pe_tile"), sem("pe_acc")
        st_hi_done, st_lo_done = sem("st_hi_done"), sem("st_lo_done")
        S = {k: sem(f"s_{k}") for k in STAGES}
        (k_mm, k_hi_done, k_lo_done, q_mm, q_hi_done, q_lo_done, s_mm, s_copied, max_done, negmax,
         exped, t_mm, ph_done, pl_done, pv_mm, bt_done, oh_mm, ct_done, og_mm, lsum_done, lrec_done,
         lg_done, o1_done, o2_done, sa_done, ga_done, mva_done, fin_ve, fin_std, fin_rc, fin_nmr,
         fin_x) = (sem(n) for n in (
            "k_mm k_hi_done k_lo_done q_mm q_hi_done q_lo_done s_mm s_copied max_done negmax "
            "exped t_mm ph_done pl_done pv_mm bt_done oh_mm ct_done og_mm lsum_done lrec_done "
            "lg_done o1_done o2_done sa_done ga_done mva_done fin_ve fin_std fin_rc fin_nmr fin_x").split())

        def cols(t, c, width=CW):
            return t[:, c * width:(c + 1) * width] if isinstance(c, int) else t[:, bass.ds(c * width, width)]

        def blocks(ap, n=CB):
            return ap.rearrange("p (b f) -> p b f", b=n)

        def spread(ap, n=CB, width=D):
            return ap.unsqueeze(2).broadcast_to([P, n, width])

        def over_blocks(ap, n=CB):
            return ap.unsqueeze(1).broadcast_to([P, n, D])

        def chunks(eng, step):
            for s in range(NSWEEP):
                step(s, 0, 0)
                step(s, 1, 1)
                with eng.Fori(0, (NC - 2) // 2) as i:
                    step(s, i * 2 + 2, 0)
                    step(s, i * 2 + 3, 1)

        def first(c):
            return isinstance(c, int) and c == 0

        def before(s, c):
            return (s - 1, NC - 1) if first(c) else (s, c - 1)

        def tile_no(s, c, g):
            return c * NS + (s * NC * NS + g)

        def landed(s, c, g):
            per = (NS - 1 - g % RAW) // RAW + 1
            return c * (16 * per) + 16 * (per * NC * s + g // RAW + 1)

        def slot_last(s, c, g):
            return tile_no(s, c, g - RAW) if g >= RAW else tile_no(s, c - 1, g + (NS - 1 - g) // RAW * RAW)

        def group(t, g):
            return t[:, g * GB * D:(g + 1) * GB * D]

        def block_of(t, b):
            return t[:, b * D:(b + 1) * D]

        def pairs(eng, pair):
            pair(0, 0, True, False)
            pair(1, 1, False, False)
            with eng.Fori(0, (NQ - 4) // 2) as i:
                pair(i * 2 + 2, 0, False, False)
                pair(i * 2 + 3, 1, False, False)
            pair(NQ - 2, 0, False, False)
            pair(NQ - 1, 1, False, True)

        SUB = [[0, 1], [2, 3]] + [[k + 2] for k in range(2, NSTEP - 2)] + [[], []]

        half = NB * D // 2
        consts = [(ident, ident_in), (comb, comb_in), (k0, w["L0_gnn_kernel"]), (w1, w["L1_gnn_W1"]),
                  (w2, w["L1_gnn_W2"]), (w3[0:H, :], w["L1_gnn_W3"]), (w3[H:2 * H, :], w["L1_gnn_W3"]),
                  (w_l2, w["L2_gnn_W"]), (w_q, w["L3_gnn_W_l"]), (w_k, w["L3_gnn_W_r"]),
                  (w_h, w["L3_gnn_W_h"]), (w_g, w["L3_gnn_W_g"]),
                  (b1, w["L1_gnn_b1"].rearrange("(h a) -> h a", a=1)),
                  (b2, w["L1_gnn_b2"].rearrange("(h a) -> h a", a=1)),
                  (bias0, w["L0_gnn_bias"].partition_broadcast(P)),
                  (bias3, w["L1_gnn_b3"].partition_broadcast(P)),
                  (bias_l2, w["L2_gnn_b"].partition_broadcast(P)),
                  (gamma, w["L3_gnn_gamma"].partition_broadcast(P)), (beta, beta_in)]
        n_const = 16 * len(consts)

        def alone(eng):
            eng.sem_inc(past_wait, 1)

        def source(s):
            return x if s in (0, 5) else v

        def wait_source(eng, s, g):
            if s == 0:
                eng.wait_ge(x_in0 if g < NG // 2 else x_in1, 16)
            elif s in (1, 2, 3):
                eng.wait_ge(S["uw"], done("uw", s - 1, g))
            elif s == 4:
                eng.wait_ge(S["vw"], done("vw", 3, g))
            else:
                eng.wait_ge(S["xw"], done("xw", 4, g))

        block = ctx.enter_context(nc.Block())

        @block.sync
        def _(sp):
            def tile(c, g):
                if isinstance(c, int):
                    return adj_t[c * NG + g]
                return adj_t[bass.ds(c * NG + g, 1)].rearrange("a p n -> (a p) n")

            def step(s, c, par):
                for g in range(NS):
                    if not (s == 0 and first(c) and g < RAW):
                        sp.wait_ge(lo_done, slot_last(s, c, g) + 1)
                    sp.dma_start(raw[:, g % RAW, :], tile(c, g)).then_inc(raw_in[g % RAW], 16)
                if s == 0:
                    if not first(c):
                        sp.wait_ge(res_in, c * 16)
                    sp.dma_start(cols(resident, c, TW), tile(c, NG - 1)).then_inc(res_in, 16)

            sp.dma_start(x[:, :half], x_in[:, :half]).then_inc(x_in0, 16)
            sp.dma_start(x[:, half:], x_in[:, half:]).then_inc(x_in1, 16)
            chunks(sp, step)
            for n in range(4):
                sp.wait_ge(fin_x, n + 1)
                sp.dma_start(cols(out, n, NB * D // 4), cols(v, n, NB * D // 4)).then_inc(out_done, 16)
            sp.wait_ge(out_done, 64)

        @block.gpsimd
        def _(pool):
            nc.gpsimd.memset(v[:], 0.0).then_inc(memset_done, 1)
            pool.wait_ge(const_in, n_const)
            pool.wait_ge(x_in0, 16)
            pool.wait_ge(x_in1, 16)

            def keep_old_x(s, c):
                if s == 5:
                    if first(c):
                        pool.wait_ge(S["resid"], done("resid", 4, NC - 1))
                    else:
                        pool.wait_ge(S["xfin"], done("xfin", 5, c) - 1)
                        pool.wait_ge(S["mm1"], done("mm1", 5, c) - 1)
                    pool.wait_ge(S["xw"], done("xw", 4, NC - 1))
                else:
                    if not (s == 0 and first(c)):
                        pool.wait_ge(S["resid"], done("resid", s, c) - 1)
                        pool.wait_ge(S["xw"], done("xw", s, c) - 1)
                alone(pool)
                if s == 0:
                    nc.gpsimd.tensor_tensor(blocks(xb[:, :]), blocks(cols(x, c)), over_blocks(bias0[:, :]),
                                            ALU.add).then_inc(S["xb"], 1)
                else:
                    nc.gpsimd.tensor_copy(xb[:, :], cols(x, c)).then_inc(S["xb"], 1)

            def step(s, c, par):
                has_before = not (s == 0 and first(c))
                ps, pc = before(s, c)
                if has_before and ps in STAGES["xb"]:
                    keep_old_x(ps, pc)
                if s == 0:
                    if not first(c):
                        pool.wait_ge(pe_acc, c)
                        alone(pool)
                    nc.gpsimd.tensor_tensor(blocks(bx[:, :]), blocks(cols(x, c)), spread(cols(beta, c, CB)),
                                            ALU.mult).then_inc(S["bx"], 1)
                if has_before and ps in STAGES["xw"]:
                    pool.wait_ge(S["norm"], done("norm", ps, pc))
                    alone(pool)
                    nc.gpsimd.tensor_copy(cols(x, pc), xn[:, :]).then_inc(S["xw"], 1)

            chunks(pool, step)
            keep_old_x(5, NC - 1)

        @block.scalar
        def _(act):
            for dst, src in consts:
                act.dma_start(dst[:, :], src).then_inc(const_in, 16)

            def stationary_hi(s, g):
                if s > 0 and g < NS:
                    act.wait_ge(pe_tile, tile_no(s - 1, NC - 1, g) + 1)
                wait_source(act, s, g)
                nc.scalar.activation(group(st_hi, g), group(source(s), g), ACT.Copy).then_inc(st_hi_done, 1)

            def evacuate(s, c, par):
                act.wait_ge(pe_acc, c + (NC * s + 1))
                if not (s == 0 and first(c)):
                    act.wait_ge(S["mm1"], done("mm1", s, c) - 1)
                rows = slice(0, 2 * H if s in NARROW else P)
                nc.scalar.activation(at[rows, :], acc[par][rows, :], ACT.Copy).then_inc(S["at"], 1)
                if s == 0:
                    nc.scalar.activation(rs_row[:, :], rs[par][0:1, :], ACT.Copy).then_inc(S["rs"], 1)

            def second(s, c):
                if s == 0:
                    act.wait_ge(S["mm1"], done("mm1", s, c))
                    nc.scalar.activation(sq[:, :], e1[:, 0:CB], ACT.Sqrt).then_inc(S["sq"], 1)
                elif s in (1, 2):
                    act.wait_ge(S["mm1"], done("mm1", s, c))
                    nc.scalar.activation(xt[0:H, :], e2[0:H, :], ACT.Relu,
                                         bias=(b1 if s == 1 else b2)[:, 0:1]).then_inc(S["h1"], 1)
                elif s == 5:
                    act.wait_ge(S["mm1"], done("mm1", s, c))
                    nc.scalar.activation(cols(v, c), e2[:, :], ACT.Copy).then_inc(S["ht"], 1)

            def deviation(s, c):
                if s in STAGES["std"]:
                    act.wait_ge(S["var"], done("var", s, c))
                    nc.scalar.activation(std[:, :], ve[:, :], ACT.Sqrt).then_inc(S["std"], 1)

            def normalise(s, c):
                if s in STAGES["norm"]:
                    act.wait_ge(S["rstd"], done("rstd", s, c))
                    if not (s == 0 and first(c)):
                        act.wait_ge(S["xw"], done("xw", s, c) - 1)
                    for b in range(CB):
                        i = nc.scalar.activation(block_of(xn, b), block_of(xs, b), ACT.Identity,
                                                 bias=nmr[:, b:b + 1], scale=rstd[:, b:b + 1])
                    i.then_inc(S["norm"], 1)

            def transposed(s, c):
                if s in STAGES["xt"]:
                    act.wait_ge(S["tx"], done("tx", s, c))
                    if not (s == 0 and first(c)):
                        act.wait_ge(S["mu"], done("mu", s, c) - 1)
                    nc.scalar.activation(xt[:, :], e2[:, :], ACT.Copy).then_inc(S["xt"], 1)

            def next_h(s, c):
                if s in STAGES["uw"]:
                    if s == 0:
                        act.wait_ge(S["mu"], done("mu", s, c))
                        if first(c):
                            act.wait_ge(memset_done, 1)
                    else:
                        act.wait_ge(S["mm2"], done("mm2", s, c))
                    nc.scalar.activation(blocks(cols(v, c))[:, :, 0:H],
                                         e3[:, 0:CB * H].rearrange("p (b h) -> p b h", b=CB),
                                         ACT.Copy).then_inc(S["uw"], 1)

            def step(s, c, par):
                has_before = not (s == 0 and first(c))
                ps, pc = before(s, c)
                for g in range(NS):
                    if first(c):
                        stationary_hi(s, g)
                    act.wait_ge(raw_in[g % RAW], landed(s, c, g))
                    if not (s == 0 and first(c) and g < 2):
                        act.wait_ge(pe_tile, tile_no(s, c, g) - 1)
                    nc.scalar.activation(t_hi[:, (par + g) % 2, :], raw[:, g % RAW, :],
                                         ACT.Copy).then_inc(hi_done, 1)
                    if has_before and g == 1:
                        evacuate(ps, pc, 1 - par)
                    if has_before and g == 2:
                        second(ps, pc)
                    if has_before and g == 3:
                        deviation(ps, pc)
                    if has_before and g == 4:
                        normalise(ps, pc)
                    if has_before and g == 6:
                        transposed(ps, pc)
                        next_h(ps, pc)

            chunks(act, step)
            stationary_hi(5, NG - 1)
            evacuate(5, NC - 1, 1)
            second(5, NC - 1)

            def keys_hi(c, e, n):
                act.wait_ge(k_mm, n + 1)
                nc.scalar.activation(cols(k_hi, c), e[:, :], ACT.Copy).then_inc(k_hi_done, 1)

            with act.Fori(0, NC // 2) as i:
                keys_hi(i * 2, e2, i * 2)
                keys_hi(i * 2 + 1, e3, i * 2 + 1)

            def query_hi(q):
                act.wait_ge(q_mm, q + 1)
                nc.scalar.activation(q_hi[:, :], e0[:, QW:2 * QW], ACT.Copy).then_inc(q_hi_done, 1)

            def exponent(q, par, rb, j):
                if j == 0 and rb == 0 and not (isinstance(q, int) and q < 2):
                    act.wait_ge(lsum_done, q - 1)
                if j == 0:
                    act.wait_ge(negmax, q * 2 + (rb + 1))
                part = pb[par][:, rb, j * EW:(j + 1) * EW]
                nc.scalar.activation(part, part, ACT.Exp, bias=nm[par][:, rb:rb + 1],
                                     accum_out=ls[par][:, rb * EQ + j:rb * EQ + j + 1]).then_inc(exped, 1)

            def pair(q, par, is_first, is_last):
                for k in range(NSTEP):
                    act.wait_ge(t_mm, q * NSTEP + (k + 1))
                    if not (is_first and k < 2):
                        act.wait_ge(pv_mm, q * NSTEP + (k - 1))
                    nc.scalar.activation(p_hi[:, k % 2, :], (e2, e3)[k % 2][:, :], ACT.Copy).then_inc(ph_done, 1)
                    if k in (1, 2):
                        exponent(q, par, 1, k + 1)
                    if not is_first and k == 1:
                        act.wait_ge(pv_mm, q * NSTEP)
                        if not (isinstance(q, int) and q < 2):
                            act.wait_ge(oh_mm, q - 1)
                        nc.scalar.activation(bt[:, :], acc[1 - par][:, 0:QW], ACT.Copy).then_inc(bt_done, 1)
                    if not is_first and k == 4:
                        act.wait_ge(oh_mm, q)
                        nc.scalar.activation(ct[:, :], e0[:, 0:QW], ACT.Copy).then_inc(ct_done, 1)
                    if not is_last and 7 <= k < 7 + EQ:
                        exponent(q + 1, 1 - par, 0, k - 7)
                    if not is_last and k == 15 and not (isinstance(q, int) and q + 2 >= NQ):
                        query_hi(q + 2)
                    if not is_last and k in (14, 15):
                        exponent(q + 1, 1 - par, 1, k - 14)

            query_hi(0)
            for j in range(EQ):
                exponent(0, 0, 0, j)
            query_hi(1)
            exponent(0, 0, 1, 0)
            exponent(0, 0, 1, 1)
            pairs(act, pair)
            act.wait_ge(pv_mm, NQ * NSTEP)
            act.wait_ge(oh_mm, NQ - 1)
            nc.scalar.activation(bt[:, :], acc[1][:, 0:QW], ACT.Copy).then_inc(bt_done, 1)
            act.wait_ge(oh_mm, NQ)
            nc.scalar.activation(ct[:, :], e0[:, 0:QW], ACT.Copy).then_inc(ct_done, 1)
            act.wait_ge(fin_ve, 1)
            nc.scalar.activation(std_a[:, :], ve_a[:, :], ACT.Sqrt).then_inc(fin_std, 1)

        @block.vector
        def _(dve):
            nc.vector.memset(ones_f[:, :], 1.0).then_inc(memset_done, 1)
            nc.vector.memset(ones_r[:, :].bitcast(F32), 1.0).then_inc(memset_done, 1)
            dve.wait_ge(const_in, n_const)

            def stationary_lo(s, g, n):
                dve.wait_ge(st_hi_done, n + 1)
                if s in NARROW:
                    hi, src = blocks(group(st_hi, g)), blocks(group(v, g))
                    nc.vector.tensor_tensor(hi[:, :, H:2 * H], src[:, :, 0:H], hi[:, :, 0:H].bitcast(F32),
                                            ALU.subtract).then_inc(st_lo_done, 1)
                else:
                    nc.vector.tensor_tensor(group(st_lo, g), group(source(s), g), group(st_hi, g).bitcast(F32),
                                            ALU.subtract).then_inc(st_lo_done, 1)

            def degrees(s, c):
                dve.wait_ge(S["sq"], done("sq", s, c))
                nc.vector.tensor_tensor(deg[:, :], e1[:, 0:CB], cols(beta, c, CB), ALU.add).then_inc(S["deg"], 1)
                nc.vector.tensor_scalar(dg2[:, :], sq[:, :], SQRT_GUARD, None, ALU.add).then_inc(S["dg2"], 1)
                dve.wait_ge(S["deg"], done("deg", s, c))
                nc.vector.reciprocal(inv[:, :], deg[:, :]).then_inc(S["inv"], 1)
                dve.wait_ge(S["dg2"], done("dg2", s, c))
                nc.vector.reciprocal(cols(dinv, c, CB), dg2[:, :]).then_inc(S["dinv0"], 1)

            def residual(s, c):
                if s in STAGES["resid"]:
                    dve.wait_ge(S["mm1"], done("mm1", s, c))
                    if not (s == 0 and first(c)):
                        dve.wait_ge(S["norm"], done("norm", s, c) - 1)
                    if s == 0:
                        degrees(s, c)
                        dve.wait_ge(S["inv"], done("inv", s, c))
                        nc.vector.tensor_tensor(blocks(xs[:, :]), blocks(e0[:, :]), spread(inv[:, :]),
                                                ALU.mult).then_inc(S["t1"], 1)
                    elif s == 3:
                        nc.vector.tensor_tensor(blocks(xs[:, :]), blocks(e0[:, :]), over_blocks(bias3[:, :]),
                                                ALU.add).then_inc(S["t1"], 1)
                    else:
                        nc.vector.tensor_tensor(blocks(xs[:, :]), blocks(e0[:, :]), spread(cols(dinv, c, CB)),
                                                ALU.mult).then_inc(S["t1"], 1)
                    dve.wait_ge(S["t1"], done("t1", s, c))
                    dve.wait_ge(S["xb"], done("xb", s, c))
                    if s == 3:
                        nc.vector.scalar_tensor_tensor(out=xs[:, :], in0=xs[:, :], scalar=0.0, in1=xb[:, :],
                                                       op0=ALU.max, op1=ALU.add).then_inc(S["t2"], 1)
                        dve.wait_ge(S["t2"], done("t2", s, c))
                        nc.vector.scalar_tensor_tensor(out=xs[:, :], in0=xs[:, :], scalar=0.0, in1=xb[:, :],
                                                       op0=ALU.max, op1=ALU.add).then_inc(S["resid"], 1)
                    else:
                        nc.vector.tensor_tensor(xs[:, :], xs[:, :], xb[:, :], ALU.add).then_inc(S["resid"], 1)
                    dve.wait_ge(S["resid"], done("resid", s, c))
                    for b in range(CB):
                        i = nc.vector.bn_stats(stats[:, b, :], block_of(xs, b))
                    i.then_inc(S["bst"], 1)
                    dve.wait_ge(S["bst"], done("bst", s, c))
                    alone(dve)
                    for b in range(CB):
                        i = nc.vector.bn_aggr(mv[:, b, :], stats[:, b, :])
                    i.then_inc(S["agg"], 1)
                    dve.wait_ge(S["agg"], done("agg", s, c))
                    nc.vector.tensor_scalar(ve[:, :], mv[:, :, 1], EPS, None, ALU.add).then_inc(S["var"], 1)
                elif s == 5:
                    dve.wait_ge(S["mm1"], done("mm1", s, c))
                    dve.wait_ge(S["xb"], done("xb", s, c))
                    nc.vector.tensor_tensor(cols(x, c), e0[:, :], xb[:, :], ALU.add).then_inc(S["xfin"], 1)

            def scales(s, c):
                if s in STAGES["rc"]:
                    dve.wait_ge(S["std"], done("std", s, c))
                    nc.vector.reciprocal(rstd[:, :], std[:, :]).then_inc(S["rc"], 1)
                    dve.wait_ge(S["rc"], done("rc", s, c))
                    nc.vector.scalar_tensor_tensor(out=nmr[:, :], in0=mv[:, :, 0], scalar=-1.0, in1=rstd[:, :],
                                                   op0=ALU.mult, op1=ALU.mult).then_inc(S["rstd"], 1)

            def laplacian_h(s, c):
                if s == 3:
                    dve.wait_ge(S["mu"], done("mu", s, c))
                    nc.vector.tensor_tensor(blocks(xs[:, :]), blocks(e3[:, :]), over_blocks(bias_l2[:, :]),
                                            ALU.add).then_inc(S["vt"], 1)
                    dve.wait_ge(S["vt"], done("vt", s, c))
                    nc.vector.tensor_tensor(blocks(cols(v, c)), blocks(xs[:, :]), spread(cols(dinv, c, CB)),
                                            ALU.mult).then_inc(S["vw"], 1)

            def step(s, c, par):
                has_before = not (s == 0 and first(c))
                ps, pc = before(s, c)
                for g in range(NS):
                    if first(c):
                        stationary_lo(s, g, s * NS + g)
                    dve.wait_ge(hi_done, tile_no(s, c, g) + 1)
                    nc.vector.tensor_tensor(t_lo[:, (par + g) % 2, :], raw[:, g % RAW, :],
                                            t_hi[:, (par + g) % 2, :].bitcast(F32),
                                            ALU.subtract).then_inc(lo_done, 1)
                    if has_before and g == 2:
                        residual(ps, pc)
                    if has_before and g == 3:
                        scales(ps, pc)
                    if has_before and g == 6:
                        laplacian_h(ps, pc)

            chunks(dve, step)
            stationary_lo(5, NG - 1, NSWEEP * NS)
            dve.wait_ge(st_lo_done, NSWEEP * NS + 1)
            residual(5, NC - 1)

            def keys_lo(c, e, n):
                dve.wait_ge(k_hi_done, n + 1)
                nc.vector.tensor_tensor(cols(k_lo, c), e[:, :], cols(k_hi, c).bitcast(F32),
                                        ALU.subtract).then_inc(k_lo_done, 1)

            with dve.Fori(0, NC // 2) as i:
                keys_lo(i * 2, e2, i * 2)
                keys_lo(i * 2 + 1, e3, i * 2 + 1)

            def query_lo(q):
                dve.wait_ge(q_hi_done, q + 1)
                nc.vector.tensor_tensor(q_lo[:, :], e0[:, QW:2 * QW], q_hi[:, :].bitcast(F32),
                                        ALU.subtract).then_inc(q_lo_done, 1)

            def scores(q, par, u):
                rb, j = divmod(u, NC)
                dve.wait_ge(s_mm, q * (QB * NC) + (u + 1))
                nc.vector.tensor_scalar(pb[par][:, rb, j * CW:(j + 1) * CW], rs[u % 2][:, :], 1.0, None, ALU.mult,
                                        ALU.max, accum_out=mx[par][:, u:u + 1]).then_inc(s_copied, 1)
                if j == NC - 1:
                    dve.wait_ge(s_copied, q * (QB * NC) + (u + 1))
                    nc.vector.reduce_max(mxr[:, rb:rb + 1], mx[par][:, rb * NC:(rb + 1) * NC],
                                         AX_X).then_inc(max_done, 1)
                    dve.wait_ge(max_done, q * QB + (rb + 1))
                    nc.vector.tensor_scalar(nm[par][:, rb:rb + 1], mxr[:, rb:rb + 1], -1.0, None,
                                            ALU.mult).then_inc(negmax, 1)

            def finish(q, par):
                dve.wait_ge(exped, (q + 1) * (QB * EQ))
                nc.vector.reduce_sum(lsum[:, :], ls[par][:, :].rearrange("p (b j) -> p b j", b=QB),
                                     AX_X).then_inc(lsum_done, 1)
                dve.wait_ge(lsum_done, q + 1)
                nc.vector.reciprocal(lrec[:, :], lsum[:, :]).then_inc(lrec_done, 1)
                dve.wait_ge(lrec_done, q + 1)
                nc.vector.tensor_scalar(lg[:, :], lrec[:, :], gamma[:, 0:1], None, ALU.mult).then_inc(lg_done, 1)
                dve.wait_ge(lg_done, q + 1)
                dve.wait_ge(og_mm, q + 1)
                nc.vector.tensor_tensor(blocks(o_s[:, :], QB), blocks(e1[:, 0:QW], QB), spread(lg[:, :], QB),
                                        ALU.mult).then_inc(o1_done, 1)
                dve.wait_ge(o1_done, q + 1)
                nc.vector.tensor_tensor(cols(x, q, QW), o_s[:, :], cols(x, q, QW), ALU.add).then_inc(o2_done, 1)
                dve.wait_ge(o2_done, q + 1)
                for b in range(QB):
                    i = nc.vector.bn_stats(stats_a[:, b, :], cols(x, q * QB + b, D))
                i.then_inc(sa_done, 1)
                dve.wait_ge(sa_done, q + 1)
                alone(dve)
                for b in range(QB):
                    i = nc.vector.bn_aggr(mv_a[:, b, :], stats_a[:, b, :])
                i.then_inc(ga_done, 1)
                dve.wait_ge(ga_done, q + 1)
                nc.vector.tensor_copy(cols(mv_all, q, 2 * QB), mv_a[:, :, :].rearrange("p b t -> p (b t)")).then_inc(
                    mva_done, 1)

            def pair(q, par, is_first, is_last):
                for k in range(NSTEP):
                    dve.wait_ge(ph_done, q * NSTEP + (k + 1))
                    nc.vector.tensor_tensor(p_lo[:, k % 2, :], (e2, e3)[k % 2][:, :],
                                            p_hi[:, k % 2, :].bitcast(F32), ALU.subtract).then_inc(pl_done, 1)
                    if not is_last:
                        for u in SUB[k]:
                            scores(q + 1, 1 - par, u)
                    if not is_first and k == 6:
                        finish(q - 1, 1 - par)
                    if not is_last and k == 15 and not (isinstance(q, int) and q + 2 >= NQ):
                        query_lo(q + 2)

            query_lo(0)
            for u in range(QB * NC):
                scores(0, 0, u)
            query_lo(1)
            pairs(dve, pair)
            finish(NQ - 1, 1)
            dve.wait_ge(mva_done, NQ)
            mva = mv_all[:, :].rearrange("p (b t) -> p b t", t=2)
            nc.vector.tensor_scalar(ve_a[:, :], mva[:, :, 1], EPS, None, ALU.add).then_inc(fin_ve, 1)
            dve.wait_ge(fin_std, 1)
            nc.vector.reciprocal(rstd_a[:, :], std_a[:, :]).then_inc(fin_rc, 1)
            dve.wait_ge(fin_rc, 1)
            nc.vector.scalar_tensor_tensor(out=nmr_a[:, :], in0=mva[:, :, 0], scalar=-1.0, in1=rstd_a[:, :],
                                           op0=ALU.mult, op1=ALU.mult).then_inc(fin_nmr, 1)
            dve.wait_ge(fin_nmr, 1)
            for b in range(NB):
                i = nc.vector.tensor_scalar(block_of(v, b), block_of(x, b), rstd_a[:, b:b + 1], nmr_a[:, b:b + 1],
                                            ALU.mult, ALU.add)
                if b % (NB // 4) == NB // 4 - 1:
                    i.then_inc(fin_x, 1)

        @block.tensor
        def _(pe):
            pe.wait_ge(const_in, n_const)
            pe.wait_ge(memset_done, 3)
            mm = nc.tensor.matmul

            def epilogue_1(s, c, par):
                pe.wait_ge(S["at"], done("at", s, c))
                if s == 0:
                    pe.wait_ge(S["rs"], done("rs", s, c))
                    for b in range(CB):
                        mm(e0[:, b * D:(b + 1) * D], block_of(at, b), k0[:, :], start=True, stop=True)
                    for b in range(CB):
                        i = mm(e1[:, b:b + 1], rs_row[0:1, b * P:(b + 1) * P], ones_f[0:1, 0:1],
                               start=True, stop=True)
                elif s in (1, 2):
                    i = mm(e2[:, :], comb[:, :], at[0:2 * H, :], start=True, stop=True)
                elif s == 3:
                    for b in range(CB):
                        i = mm(e0[:, b * D:(b + 1) * D], at[0:2 * H, b * P:(b + 1) * P], w3[:, :],
                               start=True, stop=True)
                else:
                    if s == 4:
                        pe.wait_ge(S["t1"], done("t1", 4, c) - 1)
                    elif first(c):
                        pe.wait_ge(S["t1"], done("t1", 4, NC - 1))
                    else:
                        pe.wait_ge(S["xfin"], done("xfin", 5, c) - 1)
                    for b in range(CB):
                        i = mm(e0[:, b * D:(b + 1) * D], block_of(at, b), ident[:, :], is_transpose=True,
                               start=True, stop=True)
                    if s == 5:
                        if not first(c):
                            pe.wait_ge(S["ht"], done("ht", 5, c) - 1)
                        pe.wait_ge(S["xb"], done("xb", 5, c))
                        for b in range(CB):
                            i = mm(e2[:, b * D:(b + 1) * D], block_of(xb, b), ident[:, :], is_transpose=True,
                                   start=True, stop=True)
                i.then_inc(S["mm1"], 1)

            def epilogue_2(s, c):
                if s in (1, 2):
                    pe.wait_ge(S["h1"], done("h1", s, c))
                    pe.wait_ge(S["uw"], done("uw", s, c) - 1)
                    for b in range(CB):
                        i = mm(e3[:, b * H:(b + 1) * H], xt[0:H, b * P:(b + 1) * P],
                               w2[:, :] if s == 1 else ident[0:H, 0:H], start=True, stop=True)
                    i.then_inc(S["mm2"], 1)

            def epilogue_3(s, c):
                if s in (0, 3):
                    pe.wait_ge(S["norm"], done("norm", s, c))
                    for b in range(CB):
                        i = mm(e2[:, b * D:(b + 1) * D], block_of(xn, b), ident[:, :], is_transpose=True,
                               start=True, stop=True)
                    i.then_inc(S["tx"], 1)

            def epilogue_4(s, c):
                if s in (0, 3):
                    pe.wait_ge(S["xt"], done("xt", s, c))
                    if s == 0 and not first(c):
                        pe.wait_ge(S["uw"], done("uw", 0, c) - 1)
                    if s == 3:
                        if first(c):
                            pe.wait_ge(S["uw"], done("uw", 2, NC - 1))
                        else:
                            pe.wait_ge(S["vt"], done("vt", 3, c) - 1)
                    wide, rhs = (H, w1) if s == 0 else (D, w_l2)
                    for b in range(CB):
                        i = mm(e3[:, b * wide:(b + 1) * wide], block_of(xt, b), rhs[:, :], start=True, stop=True)
                    i.then_inc(S["mu"], 1)

            def step(s, c, par):
                has_before = not (s == 0 and first(c))
                ps, pc = before(s, c)
                a, r = acc[par], rs[par]
                if not (s == 0 and isinstance(c, int) and c < 2):
                    pe.wait_ge(S["at"], done("at", s, c) - 2)
                    if s == 0:
                        pe.wait_ge(S["rs"], done("rs", s, c) - 2)
                for g in range(NS):
                    hi, lo = t_hi[:, (par + g) % 2, :], t_lo[:, (par + g) % 2, :]
                    if first(c):
                        pe.wait_ge(st_lo_done, s * NS + g + 1)
                    pe.wait_ge(hi_done, tile_no(s, c, g) + 1)
                    for j in range(GB):
                        b, m = g * GB + j, slice(j * CW, (j + 1) * CW)
                        mm(a[:, :], block_of(st_hi, b), hi[:, m], start=(b == 0), stop=False)
                        if s not in NARROW:
                            mm(a[:, :], block_of(st_lo, b), hi[:, m], start=False, stop=False)
                        if s == 0:
                            mm(r[:, :], ones_r[:, :], hi[:, m], start=(b == 0), stop=False)
                    pe.wait_ge(lo_done, tile_no(s, c, g) + 1)
                    for j in range(GB):
                        b, m = g * GB + j, slice(j * CW, (j + 1) * CW)
                        if s == 0:
                            mm(r[:, :], ones_r[:, :], lo[:, m], start=False, stop=False)
                        i = mm(a[:, :], block_of(st_hi, b), lo[:, m], start=False, stop=False)
                    i.then_inc(pe_tile, 1)
                    if has_before and g == 0:
                        epilogue_1(ps, pc, 1 - par)
                    if has_before and g == 2:
                        epilogue_2(ps, pc)
                    if has_before and g == 4:
                        epilogue_3(ps, pc)
                    if has_before and g == 6:
                        epilogue_4(ps, pc)
                if first(c):
                    wait_source(pe, s, NG - 1)
                if s == 0:
                    pe.wait_ge(res_in, c * 16 + 16)
                    pe.wait_ge(S["bx"], done("bx", 0, c))
                    for b in range(CB):
                        mm(a[:, b * D:(b + 1) * D], block_of(bx, b), ident[:, :], start=False, stop=False)
                tile = cols(resident, c, TW)
                for j in range(GB):
                    b, m = NS * GB + j, slice(j * CW, (j + 1) * CW)
                    if isinstance(c, int):
                        moving = resident[:, c * TW + j * CW:c * TW + (j + 1) * CW]
                    else:
                        moving = resident[:, bass.ds(c * TW + j * CW, CW)]
                    if s == 0:
                        mm(r[:, :], ones_f[:, :], moving, start=False, stop=(j == GB - 1))
                    i = mm(a[:, :], block_of(source(s), b), moving, start=False, stop=(j == GB - 1))
                i.then_inc(pe_acc, 1)

            chunks(pe, step)
            epilogue_1(5, NC - 1, 1)

            pe.wait_ge(S["ht"], done("ht", 5, NC - 1))
            pe.wait_ge(st_lo_done, NSWEEP * NS + 1)

            def keys(c, e, n):
                if not isinstance(n, int):
                    pe.wait_ge(k_lo_done, n - 1)
                mm(e[:, :], w_k[:, :], cols(v, c), start=True, stop=True).then_inc(k_mm, 1)

            keys(0, e2, 0)
            keys(1, e3, 1)
            with pe.Fori(0, NC // 2 - 1) as i:
                keys(i * 2 + 2, e2, i * 2 + 2)
                keys(i * 2 + 3, e3, i * 2 + 3)
            pe.wait_ge(k_lo_done, NC)

            def query(q):
                if isinstance(q, int) and q == 0:
                    pe.wait_ge(S["xfin"], done("xfin", 5, NC - 1))
                elif isinstance(q, int) and q == 1:
                    pe.wait_ge(q_lo_done, 1)
                elif not (isinstance(q, int) and q == 2):
                    pe.wait_ge(ct_done, q - 2)
                mm(e0[:, QW:2 * QW], w_q[:, :], cols(v, q, QW), start=True, stop=True).then_inc(q_mm, 1)

            def scores(q, u):
                rb, j = divmod(u, NC)
                if u == 0:
                    pe.wait_ge(q_lo_done, q + 1)
                if not (isinstance(q, int) and q == 0 and u < 2):
                    pe.wait_ge(s_copied, q * (QB * NC) + (u - 1))
                qh, ql = block_of(q_hi, rb), block_of(q_lo, rb)
                kh, kl = cols(k_hi, j), cols(k_lo, j)
                mm(rs[u % 2][:, :], qh, kh, start=True, stop=False)
                mm(rs[u % 2][:, :], qh, kl, start=False, stop=False)
                mm(rs[u % 2][:, :], ql, kh, start=False, stop=True).then_inc(s_mm, 1)

            def weighted(q, par, k):
                pe.wait_ge(pl_done, q * NSTEP + (k + 1))
                if k == 0 and not (isinstance(q, int) and q < 2):
                    pe.wait_ge(bt_done, q - 1)
                o = acc[par][:, 0:QW]
                for u in range(2):
                    b = 2 * k + u
                    ph, pl = p_hi[:, k % 2, u * QW:(u + 1) * QW], p_lo[:, k % 2, u * QW:(u + 1) * QW]
                    mm(o, block_of(st_hi, b), ph, start=(b == 0), stop=False)
                    mm(o, block_of(st_hi, b), pl, start=False, stop=False)
                    i = mm(o, block_of(st_lo, b), ph, start=False, stop=(b == NB - 1))
                i.then_inc(pv_mm, 1)

            def out_h(q):
                pe.wait_ge(bt_done, q + 1)
                mm(e0[:, 0:QW], w_h[:, :], bt[:, :], start=True, stop=True).then_inc(oh_mm, 1)

            def out_g(q):
                pe.wait_ge(ct_done, q + 1)
                if not (isinstance(q, int) and q == 0):
                    pe.wait_ge(o1_done, q)
                for b in range(QB):
                    i = mm(e1[:, b * D:(b + 1) * D], block_of(ct, b), w_g[:, :], start=True, stop=True)
                i.then_inc(og_mm, 1)

            def pair(q, par, is_first, is_last):
                for k in range(NSTEP):
                    if k % 4 == 0:
                        pe.wait_ge(exped, q * (QB * EQ) + (EQ + k // 4 + 1))
                    if not (is_first and k < 2):
                        pe.wait_ge(pl_done, q * NSTEP + (k - 1))
                    e = (e2, e3)[k % 2]
                    for u in range(2):
                        for rb in range(QB):
                            col = (2 * k + u) * P
                            i = mm(e[:, u * QW + rb * P:u * QW + (rb + 1) * P], pb[par][:, rb, col:col + P],
                                   ident[:, :], is_transpose=True, start=True, stop=True)
                    i.then_inc(t_mm, 1)
                    if not is_last:
                        for u in SUB[k]:
                            scores(q + 1, u)
                    if k > 0:
                        weighted(q, par, k - 1)
                    elif not is_first:
                        weighted(q - 1, 1 - par, NSTEP - 1)
                    if not is_first and k == 3:
                        out_h(q - 1)
                    if not is_first and k == 5:
                        out_g(q - 1)
                    if not is_last and k == 14 and not (isinstance(q, int) and q + 2 >= NQ):
                        query(q + 2)

            query(0)
            for u in range(QB * NC):
                scores(0, u)
            query(1)
            pairs(pe, pair)
            weighted(NQ - 1, 1, NSTEP - 1)
            out_h(NQ - 1)
            out_g(NQ - 1)


INPUTS = ["beta", "L0_gnn_kernel", "L0_gnn_bias", "L1_gnn_W1", "L1_gnn_b1", "L1_gnn_W2", "L1_gnn_b2", "L1_gnn_W3",
          "L1_gnn_b3", "L2_gnn_W", "L2_gnn_b", "L3_gnn_W_l", "L3_gnn_W_r", "L3_gnn_W_h", "L3_gnn_W_g",
          "L3_gnn_gamma"]


def kernel(**inputs):
    import concourse.bacc as bacc
    from concourse.bass_utils import run_bass_kernel_spmd

    nc = bacc.Bacc("TRN2", target_bir_lowering=False, num_devices=1, dynamic_dma_scratch_size=1024)
    adj = np.asarray(inputs["adj"]).reshape(P, NC, CB, P, NG, GB).transpose(1, 4, 3, 5, 2, 0)
    arrays = {
        "adj": np.ascontiguousarray(adj).reshape(NC * NG, P, TW),
        "x": np.ascontiguousarray(inputs["x"]).reshape(P, NB * D),
        "beta": np.ascontiguousarray(inputs["L0_gnn_beta"]).reshape(P, NB),
        "ident": np.eye(P, dtype=np.float32),
        "comb": np.concatenate([np.eye(H, P, dtype=np.float32)] * 2),
    }
    for name in INPUTS[1:]:
        arrays[name] = np.ascontiguousarray(inputs[name])
    aps = {k: nc.dram_tensor(f"in_{k}", a.shape, F32, kind="ExternalInput").ap() for k, a in arrays.items()}
    out = nc.dram_tensor("out", (P, NB * D), F32, kind="ExternalOutput").ap()
    build(nc, aps["adj"], aps["x"], aps["beta"], aps["ident"], aps["comb"], aps, out)
    r = run_bass_kernel_spmd(nc, [{f"in_{k}": a for k, a in arrays.items()}], core_ids=[0])
    return np.asarray(r.results[0]["out"]).reshape(N, D)
```

```python
from contextlib import ExitStack

import numpy as np

import concourse.bass as bass
from concourse import mybir

F32 = mybir.dt.float32
F32R = mybir.dt.float32r
ALU = mybir.AluOpType
ACT = mybir.ActivationFunctionType
AX_X = mybir.AxisListType.X

P = 128
N = 4096
D = 128
H = 20
NB = N // P
CB = 4
CW = CB * P
NC = NB // CB
GB = 2
NG = NB // GB
RB = 4
NS = NG - RB // GB
TW = GB * CW
NSWEEP = 6
NARROW = (1, 2, 3)
FIRST_SUMMED = 0
ADDS = ((1, 1), (2, 2), (3, 3), (6, "res0"), (8, 8), (9, 9), (10, 10), (11, 11), (12, "res1"))
SUMMED = (FIRST_SUMMED,) + tuple(t for _, t in ADDS if isinstance(t, int))
NSUM = len(ADDS)
FIRST_ONES = min(g for g in range(NS) if g not in SUMMED)
KEPT_AFTER = (3, 6, 9, NS - 1)
RW = RB * CW
RAW = 8
HL = 4
XP = 4
EPS = 1e-5
SQRT_GUARD = 1e-8
QB = 2
QW = QB * P
NQ = NB // QB
NSTEP = NB // 2
EQ = 4
EW = N // EQ

STAGES = {
    "xb": (0, 3, 4, 5), "bx": (0,), "xw": (0, 3, 4), "at": range(6), "rs": (0,), "sq": (0,),
    "h1": (1, 2), "dinv0": (0,), "deg": (0,), "inv": (0,), "dg2": (0,), "t1": (0, 3, 4),
    "resid": (0, 3, 4), "bst": (0, 3, 4), "agg": (0, 3, 4), "var": (0, 3, 4), "std": (0, 3, 4),
    "rc": (0, 3, 4), "rstd": (0, 3, 4), "norm": (0, 3, 4), "xt": (0, 3), "ht": (5,), "uw": (0, 1, 2),
    "vw": (3,), "xfin": (5,), "mm1": range(6), "rr": (0,), "mm2": (1, 2), "tx": (0, 3), "mu": (0, 3),
}


def done(stage, s, c):
    return c + (1 + NC * sum(q < s for q in STAGES[stage]))


def build(nc, adj_s, adj_r, x_dram, beta_in, ident_in, comb_in, w, out):
    with ExitStack() as ctx:
        def sb(name, shape, dt=F32, on=ctx):
            return on.enter_context(nc.sbuf_tensor(name, shape, dt))

        def bank(name):
            return ctx.enter_context(nc.psum_tensor(name, [P, CW], F32))

        ident = sb("ident", [P, P])
        comb = sb("comb", [2 * H, P])
        ones_f = sb("ones_f", [P, P])
        ones_r = sb("ones_r", [P, P], F32R)
        k0 = sb("k0", [P, D])
        w1 = sb("w1", [P, H])
        w2 = sb("w2", [H, H])
        w3 = sb("w3", [2 * H, D])
        w_l2 = sb("w_l2", [P, D])
        w_q, w_k, w_h, w_g = (sb(n, [P, D]) for n in ("w_q", "w_k", "w_h", "w_g"))
        bias0 = sb("bias0", [P, D])
        bias3, bias_l2 = sb("bias3", [1, D]), sb("bias_l2", [1, D])
        b1, b2 = sb("b1", [H, 1]), sb("b2", [H, 1])
        gamma = sb("gamma", [P, 1])
        beta = sb("beta", [P, NB])
        dinv = sb("dinv", [P, NB])
        rs_row = sb("rs_row", [1, CW])
        sq, deg, inv, dg2 = (sb(n, [P, CB]) for n in ("sq", "deg", "inv", "dg2"))
        stats = sb("stats", [P, CB, 6])
        mv = sb("mv", [P, CB, 2])
        ve, std, rstd, nmr = (sb(n, [P, CB]) for n in ("ve", "std", "rstd", "nmr"))
        mv_all = sb("mv_all", [P, NB * 2])

        x = sb("x", [P, NB * D])
        v = sb("v", [P, NB * D])
        st_hi = sb("st_hi", [P, NB * D], F32R)
        st_lo = sb("st_lo", [P, NB * D], F32R)

        with ExitStack() as swp:
            resident = sb("resident", [P, NC * RW], F32, swp)
            raw = sb("raw", [P, RAW, TW], F32, swp)
            t_hi = sb("t_hi", [P, HL, TW], F32R, swp)
            t_lo = sb("t_lo", [P, HL, TW], F32R, swp)
            at = sb("at", [P, CW], F32, swp)
            xt = sb("xt", [P, CW], F32, swp)
            xb = sb("xb", [P, CW], F32, swp)
            xs = sb("xs", [P, CW], F32, swp)
            xn = sb("xn", [P, CW], F32, swp)
            bx = sb("bx", [P, CW], F32, swp)
            rsum = sb("rsum", [P, TW], F32, swp)

        with ExitStack() as att:
            pb = [sb(f"pb{i}", [P, QB, N], F32, att) for i in range(2)]
            k_hi = sb("k_hi", [P, N], F32R, att)
            k_lo = sb("k_lo", [P, N], F32R, att)
            q_hi = sb("q_hi", [P, QW], F32R, att)
            q_lo = sb("q_lo", [P, QW], F32R, att)
            p_hi = sb("p_hi", [P, 2, 2 * QW], F32R, att)
            p_lo = sb("p_lo", [P, 2, 2 * QW], F32R, att)
            bt = sb("bt", [P, QW], F32, att)
            ct = sb("ct", [P, QW], F32, att)
            o_s = sb("o_s", [P, QW], F32, att)
            mx = [sb(f"mx{i}", [P, QB * NC], F32, att) for i in range(2)]
            mxr = sb("mxr", [P, QB], F32, att)
            nm = [sb(f"nm{i}", [P, QB], F32, att) for i in range(2)]
            ls = [sb(f"ls{i}", [P, QB * EQ], F32, att) for i in range(2)]
            lsum, lrec, lg = (sb(n, [P, QB], F32, att) for n in ("lsum", "lrec", "lg"))
            stats_a = sb("stats_a", [P, QB, 6], F32, att)
            mv_a = sb("mv_a", [P, QB, 2], F32, att)
            ve_a, std_a, rstd_a, nmr_a = (sb(n, [P, NB], F32, att) for n in ("ve_a", "std_a", "rstd_a", "nmr_a"))

        acc = [bank("acc0"), bank("acc1")]
        rs = [bank("rs0"), bank("rs1")]
        e0, e1, e2, e3 = (bank(f"e{i}") for i in range(4))

        def sem(name):
            return ctx.enter_context(nc.semaphore(name))

        past_wait = sem("past_wait")
        const_in, memset_done, out_done = sem("const_in"), sem("memset_done"), sem("out_done")
        x_in = [sem(f"x_in{i}") for i in range(XP)]
        raw_in = [sem(f"raw_in{i}") for i in range(RAW)]
        res_in = sem("res_in")
        hi_done, lo_done, pe_tile, pe_acc, sum_done = sem("hi_done"), sem("lo_done"), sem("pe_tile"), sem("pe_acc"), sem("sum_done")
        st_hi_done, st_lo_done = sem("st_hi_done"), sem("st_lo_done")
        S = {k: sem(f"s_{k}") for k in STAGES}
        (k_mm, k_hi_done, k_lo_done, q_mm, q_hi_done, q_lo_done, s_mm, s_copied, max_done, negmax,
         exped, t_mm, ph_done, pl_done, pv_mm, bt_done, oh_mm, ct_done, og_mm, lsum_done, lrec_done,
         lg_done, o1_done, o2_done, sa_done, ga_done, mva_done, fin_ve, fin_std, fin_rc, fin_nmr,
         fin_x) = (sem(n) for n in (
            "k_mm k_hi_done k_lo_done q_mm q_hi_done q_lo_done s_mm s_copied max_done negmax "
            "exped t_mm ph_done pl_done pv_mm bt_done oh_mm ct_done og_mm lsum_done lrec_done "
            "lg_done o1_done o2_done sa_done ga_done mva_done fin_ve fin_std fin_rc fin_nmr fin_x").split())

        def cols(t, c, width=CW):
            return t[:, c * width:(c + 1) * width] if isinstance(c, int) else t[:, bass.ds(c * width, width)]

        def blocks(ap, n=CB):
            return ap.rearrange("p (b f) -> p b f", b=n)

        def spread(ap, n=CB, width=D):
            return ap.unsqueeze(2).broadcast_to([P, n, width])

        def over_blocks(ap, n=CB):
            return ap.unsqueeze(1).broadcast_to([P, n, D])

        def chunks(eng, step):
            for s in range(NSWEEP):
                step(s, 0, 0)
                step(s, 1, 1)
                with eng.Fori(0, (NC - 2) // 2) as i:
                    step(s, i * 2 + 2, 0)
                    step(s, i * 2 + 3, 1)

        def first(c):
            return isinstance(c, int) and c == 0

        def before(s, c):
            return (s - 1, NC - 1) if first(c) else (s, c - 1)

        def tile_no(s, c, g):
            return c * NS + (NC * NS * s + g)

        def landed(s, c, g):
            per = (NS - 1 - g % RAW) // RAW + 1
            return c * (16 * per) + 16 * (per * NC * s + g // RAW + 1)

        def wait_slot(sp, s, c, g):
            if g >= RAW:
                qs, qc, qg = s, c, g - RAW
            else:
                qs, qc = before(s, c)
                qg = g + (NS - 1 - g) // RAW * RAW
            if qs == 0 and qg in SUMMED:
                n = [t for _, t in ADDS].index(qg or ADDS[0][1])
                sp.wait_ge(sum_done, qc * NSUM + (n + 1))
            else:
                sp.wait_ge(lo_done, tile_no(qs, qc, qg) + 1)

        def group(t, g):
            return t[:, g * GB * D:(g + 1) * GB * D]

        def block_of(t, b):
            return t[:, b * D:(b + 1) * D]

        def pairs(eng, pair):
            pair(0, 0, True, False)
            pair(1, 1, False, False)
            with eng.Fori(0, (NQ - 4) // 2) as i:
                pair(i * 2 + 2, 0, False, False)
                pair(i * 2 + 3, 1, False, False)
            pair(NQ - 2, 0, False, False)
            pair(NQ - 1, 1, False, True)

        SUB = [[0, 1], [2], [3], [4], [5], [6], [7], [8, 9], [10], [11], [12], [13], [14], [15], [], []]
        EXP_OWN = {1: (1, 0), 2: (1, 1), 4: (2, 0), 6: (2, 1), 8: (3, 0), 10: (3, 1)}
        EXP_NEXT = {12: (0, 0), 15: (0, 1)}

        consts = [(ident, ident_in), (comb, comb_in), (k0, w["L0_gnn_kernel"]), (w1, w["L1_gnn_W1"]),
                  (w2, w["L1_gnn_W2"]), (w3[0:H, :], w["L1_gnn_W3"]), (w3[H:2 * H, :], w["L1_gnn_W3"]),
                  (w_l2, w["L2_gnn_W"]), (w_q, w["L3_gnn_W_l"]), (w_k, w["L3_gnn_W_r"]),
                  (w_h, w["L3_gnn_W_h"]), (w_g, w["L3_gnn_W_g"]),
                  (b1, w["L1_gnn_b1"].rearrange("(h a) -> h a", a=1)),
                  (b2, w["L1_gnn_b2"].rearrange("(h a) -> h a", a=1)),
                  (bias0, w["L0_gnn_bias"].partition_broadcast(P)),
                  (bias3, w["L1_gnn_b3"].rearrange("(a f) -> a f", a=1)),
                  (bias_l2, w["L2_gnn_b"].rearrange("(a f) -> a f", a=1)),
                  (gamma, w["L3_gnn_gamma"].partition_broadcast(P)), (beta, beta_in)]
        n_const = 16 * len(consts)

        def alone(eng):
            eng.sem_inc(past_wait, 1)

        def source(s):
            return x if s in (0, 5) else v

        def wait_source(eng, s, g):
            if s == 0:
                eng.wait_ge(x_in[g * XP // NG], 16)
            elif s in (1, 2, 3):
                eng.wait_ge(S["uw"], done("uw", s - 1, g * GB // CB))
            elif s == 4:
                eng.wait_ge(S["vw"], done("vw", 3, g * GB // CB))
            else:
                eng.wait_ge(S["xw"], done("xw", 4, g * GB // CB))

        block = ctx.enter_context(nc.Block())

        @block.sync
        def _(sp):
            def tile(c, g):
                return rows(adj_s, c * NS + g)

            def rows(t, n):
                return t[n] if isinstance(n, int) else t[bass.ds(n, 1)].rearrange("a p n -> (a p) n")

            def step(s, c, par):
                for g in range(NS):
                    if s == 0 and first(c):
                        if g % 2 == 0 and g < 2 * XP:
                            part = g // 2
                            sp.dma_start(cols(x, part, NB * D // XP),
                                         cols(x_dram, part, NB * D // XP)).then_inc(x_in[part], 16)
                        if g == 6:
                            for dst, src in consts:
                                sp.dma_start(dst[:, :], src).then_inc(const_in, 16)
                    if s == 0 and g == (7 if first(c) else 0):
                        if not first(c):
                            sp.wait_ge(res_in, c * 16)
                        sp.dma_start(cols(resident, c, RW), rows(adj_r, c)).then_inc(res_in, 16)
                    if not (s == 0 and first(c) and g < RAW):
                        wait_slot(sp, s, c, g)
                    sp.dma_start(raw[:, g % RAW, :], tile(c, g)).then_inc(raw_in[g % RAW], 16)

            chunks(sp, step)
            for n in range(4):
                sp.wait_ge(fin_x, n + 1)
                sp.dma_start(cols(out, n, NB * D // 4), cols(v, n, NB * D // 4)).then_inc(out_done, 16)
            sp.wait_ge(out_done, 64)

        @block.gpsimd
        def _(pool):
            nc.gpsimd.memset(v[:], 0.0).then_inc(memset_done, 1)
            pool.wait_ge(const_in, n_const)
            for part in x_in:
                pool.wait_ge(part, 16)

            def keep_old_x(s, c):
                if s == 5:
                    if first(c):
                        pool.wait_ge(S["resid"], done("resid", 4, NC - 1))
                    else:
                        pool.wait_ge(S["xfin"], done("xfin", 5, c) - 1)
                        pool.wait_ge(S["mm1"], done("mm1", 5, c) - 1)
                    pool.wait_ge(S["xw"], done("xw", 4, NC - 1))
                else:
                    if not (s == 0 and first(c)):
                        pool.wait_ge(S["resid"], done("resid", s, c) - 1)
                        pool.wait_ge(S["xw"], done("xw", s, c) - 1)
                alone(pool)
                if s == 0:
                    nc.gpsimd.tensor_tensor(blocks(xb[:, :]), blocks(cols(x, c)), over_blocks(bias0[:, :]),
                                            ALU.add).then_inc(S["xb"], 1)
                else:
                    nc.gpsimd.tensor_copy(xb[:, :], cols(x, c)).then_inc(S["xb"], 1)

            def step(s, c, par):
                has_before = not (s == 0 and first(c))
                ps, pc = before(s, c)
                if has_before and ps in STAGES["xb"]:
                    keep_old_x(ps, pc)
                if s == 0:
                    if not first(c):
                        pool.wait_ge(pe_acc, c)
                        alone(pool)
                    nc.gpsimd.tensor_tensor(blocks(bx[:, :]), blocks(cols(x, c)), spread(cols(beta, c, CB)),
                                            ALU.mult).then_inc(S["bx"], 1)
                if has_before and ps in STAGES["xw"]:
                    pool.wait_ge(S["norm"], done("norm", ps, pc))
                    alone(pool)
                    nc.gpsimd.tensor_copy(cols(x, pc), xn[:, :]).then_inc(S["xw"], 1)

            chunks(pool, step)
            keep_old_x(5, NC - 1)

        @block.scalar
        def _(act):

            def stationary_hi(s, g):
                if s > 0 and g < NS:
                    act.wait_ge(pe_tile, tile_no(s - 1, NC - 1, g) + 1)
                wait_source(act, s, g)
                nc.scalar.activation(group(st_hi, g), group(source(s), g), ACT.Copy).then_inc(st_hi_done, 1)

            def evacuate(s, c, par):
                act.wait_ge(pe_acc, c + (NC * s + 1))
                if not (s == 0 and first(c)):
                    act.wait_ge(S["mm1"], done("mm1", s, c) - 1)
                rows = slice(0, 2 * H if s in NARROW else P)
                nc.scalar.activation(at[rows, :], acc[par][rows, :], ACT.Copy).then_inc(S["at"], 1)
                if s == 0:
                    nc.scalar.activation(rs_row[:, :], rs[par][0:1, :], ACT.Copy).then_inc(S["rs"], 1)

            def second(s, c):
                if s == 0:
                    act.wait_ge(S["mm1"], done("mm1", s, c))
                    nc.scalar.activation(sq[:, :], e1[:, 0:CB], ACT.Sqrt).then_inc(S["sq"], 1)
                elif s in (1, 2):
                    act.wait_ge(S["mm1"], done("mm1", s, c))
                    nc.scalar.activation(xt[0:H, :], e2[0:H, :], ACT.Relu,
                                         bias=(b1 if s == 1 else b2)[:, 0:1]).then_inc(S["h1"], 1)
                elif s == 5:
                    act.wait_ge(S["mm1"], done("mm1", s, c))
                    nc.scalar.activation(cols(v, c), e2[:, :], ACT.Copy).then_inc(S["ht"], 1)

            def deviation(s, c):
                if s in STAGES["std"]:
                    act.wait_ge(S["var"], done("var", s, c))
                    nc.scalar.activation(std[:, :], ve[:, :], ACT.Sqrt).then_inc(S["std"], 1)

            def normalise(s, c):
                if s in STAGES["norm"]:
                    act.wait_ge(S["rstd"], done("rstd", s, c))
                    if not (s == 0 and first(c)):
                        act.wait_ge(S["xw"], done("xw", s, c) - 1)
                    for b in range(CB):
                        i = nc.scalar.activation(block_of(xn, b), block_of(xs, b), ACT.Identity,
                                                 bias=nmr[:, b:b + 1], scale=rstd[:, b:b + 1])
                    i.then_inc(S["norm"], 1)

            def transposed(s, c):
                if s in STAGES["xt"]:
                    act.wait_ge(S["tx"], done("tx", s, c))
                    if not (s == 0 and first(c)):
                        act.wait_ge(S["mu"], done("mu", s, c) - 1)
                    nc.scalar.activation(xt[:, :], e2[:, :], ACT.Copy).then_inc(S["xt"], 1)

            def next_h(s, c):
                if s in STAGES["uw"]:
                    if s == 0:
                        act.wait_ge(S["mu"], done("mu", s, c))
                        if first(c):
                            act.wait_ge(memset_done, 1)
                    else:
                        act.wait_ge(S["mm2"], done("mm2", s, c))
                    nc.scalar.activation(blocks(cols(v, c))[:, :, 0:H],
                                         e3[:, 0:CB * H].rearrange("p (b h) -> p b h", b=CB),
                                         ACT.Copy).then_inc(S["uw"], 1)

            def step(s, c, par):
                has_before = not (s == 0 and first(c))
                ps, pc = before(s, c)
                for g in range(NS):
                    if first(c):
                        stationary_hi(s, g)
                    act.wait_ge(raw_in[g % RAW], landed(s, c, g))
                    if not (s == 0 and first(c) and g < HL):
                        act.wait_ge(pe_tile, tile_no(s, c, g) - (HL - 1))
                    nc.scalar.activation(t_hi[:, (par * NS + g) % HL, :], raw[:, g % RAW, :],
                                         ACT.Copy).then_inc(hi_done, 1)
                    if has_before:
                        if g == 2:
                            evacuate(ps, pc, 1 - par)
                        if g == 4:
                            second(ps, pc)
                        if g == 7:
                            deviation(ps, pc)
                        if g == 9:
                            normalise(ps, pc)
                        if g == 12:
                            transposed(ps, pc)
                if has_before:
                    next_h(ps, pc)

            chunks(act, step)
            for g in range(NS, NG):
                stationary_hi(5, g)
            evacuate(5, NC - 1, 1)
            second(5, NC - 1)

            def keys_hi(c, e, n):
                act.wait_ge(k_mm, n + 1)
                nc.scalar.activation(cols(k_hi, c), e[:, :], ACT.Copy).then_inc(k_hi_done, 1)

            with act.Fori(0, NC // 2) as i:
                keys_hi(i * 2, e2, i * 2)
                keys_hi(i * 2 + 1, e3, i * 2 + 1)

            def query_hi(q):
                act.wait_ge(q_mm, q + 1)
                nc.scalar.activation(q_hi[:, :], e0[:, QW:2 * QW], ACT.Copy).then_inc(q_hi_done, 1)

            def exponent(q, par, j, rb):
                if j == 0 and rb == 0 and not (isinstance(q, int) and q < 2):
                    act.wait_ge(lsum_done, q - 1)
                if j == 0:
                    act.wait_ge(negmax, q * QB + (rb + 1))
                part = pb[par][:, rb, j * EW:(j + 1) * EW]
                nc.scalar.activation(part, part, ACT.Exp, bias=nm[par][:, rb:rb + 1],
                                     accum_out=ls[par][:, rb * EQ + j:rb * EQ + j + 1]).then_inc(exped, 1)

            def pair(q, par, is_first, is_last):
                for k in range(NSTEP):
                    act.wait_ge(t_mm, q * NSTEP + (k + 1))
                    if not (is_first and k < 2):
                        act.wait_ge(pv_mm, q * NSTEP + (k - 1))
                    nc.scalar.activation(p_hi[:, k % 2, :], (e2, e3)[k % 2][:, :], ACT.Copy).then_inc(ph_done, 1)
                    if k in EXP_OWN:
                        exponent(q, par, *EXP_OWN[k])
                    if not is_last and k in EXP_NEXT:
                        exponent(q + 1, 1 - par, *EXP_NEXT[k])
                    if not is_first and k == 3:
                        act.wait_ge(pv_mm, q * NSTEP)
                        if not (isinstance(q, int) and q < 2):
                            act.wait_ge(oh_mm, q - 1)
                        nc.scalar.activation(bt[:, :], acc[1 - par][:, 0:QW], ACT.Copy).then_inc(bt_done, 1)
                    if not is_first and k == 7:
                        act.wait_ge(oh_mm, q)
                        nc.scalar.activation(ct[:, :], e0[:, 0:QW], ACT.Copy).then_inc(ct_done, 1)
                    if not is_last and k == 14 and not (isinstance(q, int) and q + 2 >= NQ):
                        query_hi(q + 2)

            query_hi(0)
            exponent(0, 0, 0, 0)
            query_hi(1)
            exponent(0, 0, 0, 1)
            pairs(act, pair)
            act.wait_ge(pv_mm, NQ * NSTEP)
            act.wait_ge(oh_mm, NQ - 1)
            nc.scalar.activation(bt[:, :], acc[1][:, 0:QW], ACT.Copy).then_inc(bt_done, 1)
            act.wait_ge(oh_mm, NQ)
            nc.scalar.activation(ct[:, :], e0[:, 0:QW], ACT.Copy).then_inc(ct_done, 1)
            act.wait_ge(fin_ve, 1)
            nc.scalar.activation(std_a[:, :], ve_a[:, :], ACT.Sqrt).then_inc(fin_std, 1)

        @block.vector
        def _(dve):
            nc.vector.memset(ones_f[:, :], 1.0).then_inc(memset_done, 1)
            nc.vector.memset(ones_r[:, :].bitcast(F32), 1.0).then_inc(memset_done, 1)

            def row_sum(c, n):
                if n == 0:
                    if not first(c):
                        dve.wait_ge(S["rr"], done("rr", 0, c) - 1)
                        dve.wait_ge(pe_acc, c)
                    nc.vector.tensor_tensor(rsum[:, :], raw[:, 0, :], raw[:, 1, :], ALU.add).then_inc(sum_done, 1)
                else:
                    dve.wait_ge(sum_done, c * NSUM + n)
                    tile = ADDS[n][1]
                    if isinstance(tile, int):
                        other = raw[:, tile % RAW, :]
                    else:
                        if tile == "res0":
                            dve.wait_ge(res_in, c * 16 + 16)
                        other = cols(resident, c * (RB // GB) + int(tile[3]), TW)
                    nc.vector.tensor_tensor(rsum[:, :], rsum[:, :], other, ALU.add).then_inc(sum_done, 1)

            def fold(c):
                dve.wait_ge(sum_done, c * NSUM + NSUM)
                nc.vector.tensor_tensor(rsum[:, 0:CW], rsum[:, 0:CW], rsum[:, CW:2 * CW],
                                        ALU.add).then_inc(S["rr"], 1)

            def stationary_lo(s, g, n):
                dve.wait_ge(st_hi_done, n + 1)
                if s in NARROW:
                    hi, src = blocks(group(st_hi, g)), blocks(group(v, g))
                    nc.vector.tensor_tensor(hi[:, :, H:2 * H], src[:, :, 0:H], hi[:, :, 0:H].bitcast(F32),
                                            ALU.subtract).then_inc(st_lo_done, 1)
                else:
                    nc.vector.tensor_tensor(group(st_lo, g), group(source(s), g), group(st_hi, g).bitcast(F32),
                                            ALU.subtract).then_inc(st_lo_done, 1)

            def degrees(s, c):
                if first(c):
                    dve.wait_ge(const_in, n_const)
                dve.wait_ge(S["sq"], done("sq", s, c))
                nc.vector.tensor_tensor(deg[:, :], e1[:, 0:CB], cols(beta, c, CB), ALU.add).then_inc(S["deg"], 1)
                nc.vector.tensor_scalar(dg2[:, :], sq[:, :], SQRT_GUARD, None, ALU.add).then_inc(S["dg2"], 1)
                dve.wait_ge(S["deg"], done("deg", s, c))
                nc.vector.reciprocal(inv[:, :], deg[:, :]).then_inc(S["inv"], 1)
                dve.wait_ge(S["dg2"], done("dg2", s, c))
                nc.vector.reciprocal(cols(dinv, c, CB), dg2[:, :]).then_inc(S["dinv0"], 1)

            def residual_1(s, c):
                if s in STAGES["resid"]:
                    dve.wait_ge(S["mm1"], done("mm1", s, c))
                    if not (s == 0 and first(c)):
                        dve.wait_ge(S["norm"], done("norm", s, c) - 1)
                    if s == 0:
                        degrees(s, c)
                        dve.wait_ge(S["inv"], done("inv", s, c))
                        nc.vector.tensor_tensor(blocks(xs[:, :]), blocks(e0[:, :]), spread(inv[:, :]),
                                                ALU.mult).then_inc(S["t1"], 1)
                    elif s == 3:
                        dve.wait_ge(S["xb"], done("xb", s, c))
                        nc.vector.scalar_tensor_tensor(out=xs[:, :], in0=e0[:, :], scalar=0.0, in1=xb[:, :],
                                                       op0=ALU.max, op1=ALU.add).then_inc(S["t1"], 1)
                    else:
                        nc.vector.tensor_tensor(blocks(xs[:, :]), blocks(e0[:, :]), spread(cols(dinv, c, CB)),
                                                ALU.mult).then_inc(S["t1"], 1)

            def residual_2(s, c):
                if s in STAGES["resid"]:
                    dve.wait_ge(S["t1"], done("t1", s, c))
                    if s == 3:
                        nc.vector.scalar_tensor_tensor(out=xs[:, :], in0=xs[:, :], scalar=0.0, in1=xb[:, :],
                                                       op0=ALU.max, op1=ALU.add).then_inc(S["resid"], 1)
                    else:
                        dve.wait_ge(S["xb"], done("xb", s, c))
                        nc.vector.tensor_tensor(xs[:, :], xs[:, :], xb[:, :], ALU.add).then_inc(S["resid"], 1)
                elif s == 5:
                    dve.wait_ge(S["mm1"], done("mm1", s, c))
                    dve.wait_ge(S["xb"], done("xb", s, c))
                    nc.vector.tensor_tensor(cols(x, c), e0[:, :], xb[:, :], ALU.add).then_inc(S["xfin"], 1)

            def statistics(s, c):
                if s in STAGES["bst"]:
                    dve.wait_ge(S["resid"], done("resid", s, c))
                    for b in range(CB):
                        i = nc.vector.bn_stats(stats[:, b, :], block_of(xs, b))
                    i.then_inc(S["bst"], 1)
                    dve.wait_ge(S["bst"], done("bst", s, c))
                    alone(dve)
                    for b in range(CB):
                        i = nc.vector.bn_aggr(mv[:, b, :], stats[:, b, :])
                    i.then_inc(S["agg"], 1)
                    dve.wait_ge(S["agg"], done("agg", s, c))
                    nc.vector.tensor_scalar(ve[:, :], mv[:, :, 1], EPS, None, ALU.add).then_inc(S["var"], 1)

            def scales(s, c):
                if s in STAGES["rc"]:
                    dve.wait_ge(S["std"], done("std", s, c))
                    nc.vector.reciprocal(rstd[:, :], std[:, :]).then_inc(S["rc"], 1)
                    dve.wait_ge(S["rc"], done("rc", s, c))
                    nc.vector.scalar_tensor_tensor(out=nmr[:, :], in0=mv[:, :, 0], scalar=-1.0, in1=rstd[:, :],
                                                   op0=ALU.mult, op1=ALU.mult).then_inc(S["rstd"], 1)

            def laplacian_h(s, c):
                if s == 3:
                    dve.wait_ge(S["mu"], done("mu", s, c))
                    nc.vector.tensor_tensor(blocks(cols(v, c)), blocks(e3[:, :]), spread(cols(dinv, c, CB)),
                                            ALU.mult).then_inc(S["vw"], 1)

            def step(s, c, par):
                has_before = not (s == 0 and first(c))
                ps, pc = before(s, c)
                for g in range(NS):
                    if first(c):
                        stationary_lo(s, g, NS * s + g)
                    dve.wait_ge(hi_done, tile_no(s, c, g) + 1)
                    nc.vector.tensor_tensor(t_lo[:, (par * NS + g) % HL, :], raw[:, g % RAW, :],
                                            t_hi[:, (par * NS + g) % HL, :].bitcast(F32),
                                            ALU.subtract).then_inc(lo_done, 1)
                    for n, (after, _) in enumerate(ADDS):
                        if s == 0 and after == g:
                            row_sum(c, n)
                    if has_before:
                        if g == 4:
                            residual_1(ps, pc)
                        if g == 5:
                            residual_2(ps, pc)
                        if g == 6:
                            statistics(ps, pc)
                        if g == 8:
                            scales(ps, pc)
                if s == 0:
                    fold(c)
                if has_before:
                    laplacian_h(ps, pc)

            chunks(dve, step)
            for g in range(NS, NG):
                stationary_lo(5, g, NSWEEP * NS + g - NS)
            dve.wait_ge(st_lo_done, NSWEEP * NS + NG - NS)
            residual_2(5, NC - 1)

            def keys_lo(c, e, n):
                dve.wait_ge(k_hi_done, n + 1)
                nc.vector.tensor_tensor(cols(k_lo, c), e[:, :], cols(k_hi, c).bitcast(F32),
                                        ALU.subtract).then_inc(k_lo_done, 1)

            with dve.Fori(0, NC // 2) as i:
                keys_lo(i * 2, e2, i * 2)
                keys_lo(i * 2 + 1, e3, i * 2 + 1)

            def query_lo(q):
                dve.wait_ge(q_hi_done, q + 1)
                nc.vector.tensor_tensor(q_lo[:, :], e0[:, QW:2 * QW], q_hi[:, :].bitcast(F32),
                                        ALU.subtract).then_inc(q_lo_done, 1)

            def scores(q, par, u):
                rb, j = divmod(u, NC)
                dve.wait_ge(s_mm, q * (QB * NC) + (u + 1))
                nc.vector.tensor_scalar(pb[par][:, rb, j * CW:(j + 1) * CW], rs[u % 2][:, :], 1.0, None, ALU.mult,
                                        ALU.max, accum_out=mx[par][:, u:u + 1]).then_inc(s_copied, 1)
                if j == NC - 1:
                    dve.wait_ge(s_copied, q * (QB * NC) + (u + 1))
                    nc.vector.reduce_max(mxr[:, rb:rb + 1], mx[par][:, rb * NC:(rb + 1) * NC],
                                         AX_X).then_inc(max_done, 1)
                    dve.wait_ge(max_done, q * QB + (rb + 1))
                    nc.vector.tensor_scalar(nm[par][:, rb:rb + 1], mxr[:, rb:rb + 1], -1.0, None,
                                            ALU.mult).then_inc(negmax, 1)

            def finish_sums(q, par):
                dve.wait_ge(exped, (q + 1) * (QB * EQ))
                nc.vector.reduce_sum(lsum[:, :], ls[par][:, :].rearrange("p (b j) -> p b j", b=QB),
                                     AX_X).then_inc(lsum_done, 1)
                dve.wait_ge(lsum_done, q + 1)
                nc.vector.reciprocal(lrec[:, :], lsum[:, :]).then_inc(lrec_done, 1)
                dve.wait_ge(lrec_done, q + 1)
                nc.vector.tensor_scalar(lg[:, :], lrec[:, :], gamma[:, 0:1], None, ALU.mult).then_inc(lg_done, 1)

            def finish_add(q):
                dve.wait_ge(lg_done, q + 1)
                dve.wait_ge(og_mm, q + 1)
                nc.vector.tensor_tensor(blocks(o_s[:, :], QB), blocks(e1[:, 0:QW], QB), spread(lg[:, :], QB),
                                        ALU.mult).then_inc(o1_done, 1)
                dve.wait_ge(o1_done, q + 1)
                nc.vector.tensor_tensor(cols(x, q, QW), o_s[:, :], cols(x, q, QW), ALU.add).then_inc(o2_done, 1)

            def finish_stats(q):
                dve.wait_ge(o2_done, q + 1)
                for b in range(QB):
                    i = nc.vector.bn_stats(stats_a[:, b, :], cols(x, q * QB + b, D))
                i.then_inc(sa_done, 1)
                dve.wait_ge(sa_done, q + 1)
                alone(dve)
                for b in range(QB):
                    i = nc.vector.bn_aggr(mv_a[:, b, :], stats_a[:, b, :])
                i.then_inc(ga_done, 1)
                dve.wait_ge(ga_done, q + 1)
                nc.vector.tensor_copy(cols(mv_all, q, 2 * QB), mv_a[:, :, :].rearrange("p b t -> p (b t)")).then_inc(
                    mva_done, 1)

            def pair(q, par, is_first, is_last):
                for k in range(NSTEP):
                    dve.wait_ge(ph_done, q * NSTEP + (k + 1))
                    nc.vector.tensor_tensor(p_lo[:, k % 2, :], (e2, e3)[k % 2][:, :],
                                            p_hi[:, k % 2, :].bitcast(F32), ALU.subtract).then_inc(pl_done, 1)
                    if not is_last:
                        for u in SUB[k]:
                            scores(q + 1, 1 - par, u)
                    if not is_first and k == 2:
                        finish_sums(q - 1, 1 - par)
                    if not is_first and k == 10:
                        finish_add(q - 1)
                    if not is_first and k == 12:
                        finish_stats(q - 1)
                    if not is_last and k == 14 and not (isinstance(q, int) and q + 2 >= NQ):
                        query_lo(q + 2)

            query_lo(0)
            for u in range(QB * NC):
                scores(0, 0, u)
            query_lo(1)
            pairs(dve, pair)
            finish_sums(NQ - 1, 1)
            finish_add(NQ - 1)
            finish_stats(NQ - 1)
            dve.wait_ge(mva_done, NQ)
            mva = mv_all[:, :].rearrange("p (b t) -> p b t", t=2)
            nc.vector.tensor_scalar(ve_a[:, :], mva[:, :, 1], EPS, None, ALU.add).then_inc(fin_ve, 1)
            dve.wait_ge(fin_std, 1)
            nc.vector.reciprocal(rstd_a[:, :], std_a[:, :]).then_inc(fin_rc, 1)
            dve.wait_ge(fin_rc, 1)
            nc.vector.scalar_tensor_tensor(out=nmr_a[:, :], in0=mva[:, :, 0], scalar=-1.0, in1=rstd_a[:, :],
                                           op0=ALU.mult, op1=ALU.mult).then_inc(fin_nmr, 1)
            dve.wait_ge(fin_nmr, 1)
            for b in range(NB):
                i = nc.vector.tensor_scalar(block_of(v, b), block_of(x, b), rstd_a[:, b:b + 1], nmr_a[:, b:b + 1],
                                            ALU.mult, ALU.add)
                if b % (NB // 4) == NB // 4 - 1:
                    i.then_inc(fin_x, 1)

        @block.tensor
        def _(pe):
            pe.wait_ge(memset_done, 3)
            mm = nc.tensor.matmul

            def epilogue_1(s, c, par):
                pe.wait_ge(S["at"], done("at", s, c))
                if s == 0:
                    pe.wait_ge(S["rs"], done("rs", s, c))
                    for b in range(CB):
                        mm(e0[:, b * D:(b + 1) * D], block_of(at, b), k0[:, :], start=True, stop=True)
                    for b in range(CB):
                        i = mm(e1[:, b:b + 1], rs_row[0:1, b * P:(b + 1) * P], ones_f[0:1, 0:1],
                               start=True, stop=True)
                elif s in (1, 2):
                    i = mm(e2[:, :], comb[:, :], at[0:2 * H, :], start=True, stop=True)
                elif s == 3:
                    for b in range(CB):
                        mm(e0[:, b * D:(b + 1) * D], ones_f[0:1, :], bias3[:, :], start=True, stop=False)
                        i = mm(e0[:, b * D:(b + 1) * D], at[0:2 * H, b * P:(b + 1) * P], w3[:, :],
                               start=False, stop=True)
                else:
                    if s == 4:
                        pe.wait_ge(S["t1"], done("t1", 4, c) - 1)
                    elif first(c):
                        pe.wait_ge(S["t1"], done("t1", 4, NC - 1))
                    else:
                        pe.wait_ge(S["xfin"], done("xfin", 5, c) - 1)
                    for b in range(CB):
                        i = mm(e0[:, b * D:(b + 1) * D], block_of(at, b), ident[:, :], is_transpose=True,
                               start=True, stop=True)
                    if s == 5:
                        if not first(c):
                            pe.wait_ge(S["ht"], done("ht", 5, c) - 1)
                        pe.wait_ge(S["xb"], done("xb", 5, c))
                        for b in range(CB):
                            i = mm(e2[:, b * D:(b + 1) * D], block_of(xb, b), ident[:, :], is_transpose=True,
                                   start=True, stop=True)
                i.then_inc(S["mm1"], 1)

            def epilogue_2(s, c):
                if s in (1, 2):
                    pe.wait_ge(S["h1"], done("h1", s, c))
                    pe.wait_ge(S["uw"], done("uw", s, c) - 1)
                    for b in range(CB):
                        i = mm(e3[:, b * H:(b + 1) * H], xt[0:H, b * P:(b + 1) * P],
                               w2[:, :] if s == 1 else ident[0:H, 0:H], start=True, stop=True)
                    i.then_inc(S["mm2"], 1)

            def epilogue_3(s, c):
                if s in (0, 3):
                    pe.wait_ge(S["norm"], done("norm", s, c))
                    for b in range(CB):
                        i = mm(e2[:, b * D:(b + 1) * D], block_of(xn, b), ident[:, :], is_transpose=True,
                               start=True, stop=True)
                    i.then_inc(S["tx"], 1)

            def epilogue_4(s, c):
                if s in (0, 3):
                    pe.wait_ge(S["xt"], done("xt", s, c))
                    if s == 0 and not first(c):
                        pe.wait_ge(S["uw"], done("uw", 0, c) - 1)
                    if s == 3:
                        if first(c):
                            pe.wait_ge(S["uw"], done("uw", 2, NC - 1))
                        else:
                            pe.wait_ge(S["vw"], done("vw", 3, c) - 1)
                    wide, rhs = (H, w1) if s == 0 else (D, w_l2)
                    for b in range(CB):
                        if s == 3:
                            mm(e3[:, b * D:(b + 1) * D], ones_f[0:1, :], bias_l2[:, :], start=True, stop=False)
                        i = mm(e3[:, b * wide:(b + 1) * wide], block_of(xt, b), rhs[:, :], start=(s == 0), stop=True)
                    i.then_inc(S["mu"], 1)

            def step(s, c, par):
                has_before = not (s == 0 and first(c))
                ps, pc = before(s, c)
                a, r = acc[par], rs[par]
                if not (s == 0 and isinstance(c, int) and c < 2):
                    pe.wait_ge(S["at"], done("at", s, c) - 2)
                    if s == 0:
                        pe.wait_ge(S["rs"], done("rs", s, c) - 2)
                for g in range(NS):
                    hi, lo = t_hi[:, (par * NS + g) % HL, :], t_lo[:, (par * NS + g) % HL, :]
                    ones_too = s == 0 and g not in SUMMED
                    if first(c):
                        pe.wait_ge(st_lo_done, NS * s + g + 1)
                    pe.wait_ge(hi_done, tile_no(s, c, g) + 1)
                    for j in range(GB):
                        b, m = g * GB + j, slice(j * CW, (j + 1) * CW)
                        mm(a[:, :], block_of(st_hi, b), hi[:, m], start=(b == 0), stop=False)
                        if s not in NARROW:
                            mm(a[:, :], block_of(st_lo, b), hi[:, m], start=False, stop=False)
                        if ones_too:
                            mm(r[:, :], ones_r[:, :], hi[:, m], start=(g == FIRST_ONES and j == 0), stop=False)
                    pe.wait_ge(lo_done, tile_no(s, c, g) + 1)
                    for j in range(GB):
                        b, m = g * GB + j, slice(j * CW, (j + 1) * CW)
                        if ones_too:
                            mm(r[:, :], ones_r[:, :], lo[:, m], start=False, stop=False)
                        i = mm(a[:, :], block_of(st_hi, b), lo[:, m], start=False, stop=False)
                    i.then_inc(pe_tile, 1)
                    if has_before:
                        if g == 1:
                            epilogue_1(ps, pc, 1 - par)
                        if g == 5:
                            epilogue_2(ps, pc)
                        if g == 8:
                            epilogue_3(ps, pc)
                        if g == 11:
                            epilogue_4(ps, pc)
                    if s == 0 and g == 4:
                        if first(c):
                            pe.wait_ge(const_in, n_const)
                        pe.wait_ge(S["bx"], done("bx", 0, c))
                        for b in range(CB):
                            mm(a[:, b * D:(b + 1) * D], block_of(bx, b), ident[:, :], start=False, stop=False)
                    if s == 0 and g == NS - 1:
                        pe.wait_ge(S["rr"], done("rr", 0, c))
                        mm(r[:, :], ones_f[:, :], rsum[:, 0:CW], start=False, stop=True)
                    if g in KEPT_AFTER and not first(c):
                        kept = [KEPT_AFTER.index(g)]
                    elif g == NS - 1:
                        kept = range(RB)
                        wait_source(pe, s, NG - 1)
                    else:
                        kept = []
                    if s == 0 and len(kept) and kept[0] == 0:
                        pe.wait_ge(res_in, c * 16 + 16)
                    for j in kept:
                        i = mm(a[:, :], block_of(source(s), NS * GB + j), cols(resident, c * RB + j),
                               start=False, stop=(j == RB - 1))
                    if g == NS - 1:
                        i.then_inc(pe_acc, 1)

            chunks(pe, step)
            epilogue_1(5, NC - 1, 1)

            pe.wait_ge(S["ht"], done("ht", 5, NC - 1))
            pe.wait_ge(st_lo_done, NSWEEP * NS + NG - NS)

            def keys(c, e, n):
                if not isinstance(n, int):
                    pe.wait_ge(k_lo_done, n - 1)
                mm(e[:, :], w_k[:, :], cols(v, c), start=True, stop=True).then_inc(k_mm, 1)

            keys(0, e2, 0)
            keys(1, e3, 1)
            with pe.Fori(0, NC // 2 - 1) as i:
                keys(i * 2 + 2, e2, i * 2 + 2)
                keys(i * 2 + 3, e3, i * 2 + 3)
            pe.wait_ge(k_lo_done, NC)

            def query(q):
                if isinstance(q, int) and q == 0:
                    pe.wait_ge(S["xfin"], done("xfin", 5, NC - 1))
                elif isinstance(q, int) and q == 1:
                    pe.wait_ge(q_lo_done, 1)
                elif not (isinstance(q, int) and q == 2):
                    pe.wait_ge(ct_done, q - 2)
                mm(e0[:, QW:2 * QW], w_q[:, :], cols(v, q, QW), start=True, stop=True).then_inc(q_mm, 1)

            def scores(q, u):
                rb, j = divmod(u, NC)
                if u == 0:
                    pe.wait_ge(q_lo_done, q + 1)
                if not (isinstance(q, int) and q == 0 and u < 2):
                    pe.wait_ge(s_copied, q * (QB * NC) + (u - 1))
                qh, ql = block_of(q_hi, rb), block_of(q_lo, rb)
                kh, kl = cols(k_hi, j), cols(k_lo, j)
                mm(rs[u % 2][:, :], qh, kh, start=True, stop=False)
                mm(rs[u % 2][:, :], qh, kl, start=False, stop=False)
                mm(rs[u % 2][:, :], ql, kh, start=False, stop=True).then_inc(s_mm, 1)

            def weighted(q, par, k):
                pe.wait_ge(pl_done, q * NSTEP + (k + 1))
                if k == 0 and not (isinstance(q, int) and q < 2):
                    pe.wait_ge(bt_done, q - 1)
                o = acc[par][:, 0:QW]
                for u in range(2):
                    b = 2 * k + u
                    ph, pl = p_hi[:, k % 2, u * QW:(u + 1) * QW], p_lo[:, k % 2, u * QW:(u + 1) * QW]
                    mm(o, block_of(st_hi, b), ph, start=(b == 0), stop=False)
                    mm(o, block_of(st_hi, b), pl, start=False, stop=False)
                    i = mm(o, block_of(st_lo, b), ph, start=False, stop=(b == NB - 1))
                i.then_inc(pv_mm, 1)

            def out_h(q):
                pe.wait_ge(bt_done, q + 1)
                mm(e0[:, 0:QW], w_h[:, :], bt[:, :], start=True, stop=True).then_inc(oh_mm, 1)

            def out_g(q):
                pe.wait_ge(ct_done, q + 1)
                if not (isinstance(q, int) and q == 0):
                    pe.wait_ge(o1_done, q)
                for b in range(QB):
                    i = mm(e1[:, b * D:(b + 1) * D], block_of(ct, b), w_g[:, :], start=True, stop=True)
                i.then_inc(og_mm, 1)

            def pair(q, par, is_first, is_last):
                for k in range(NSTEP):
                    if k % 4 == 0:
                        pe.wait_ge(exped, q * (QB * EQ) + QB * (k // EQ + 1))
                    if not (is_first and k < 2):
                        pe.wait_ge(pl_done, q * NSTEP + (k - 1))
                    e = (e2, e3)[k % 2]
                    for u in range(2):
                        for rb in range(QB):
                            col = (2 * k + u) * P
                            i = mm(e[:, u * QW + rb * P:u * QW + (rb + 1) * P], pb[par][:, rb, col:col + P],
                                   ident[:, :], is_transpose=True, start=True, stop=True)
                    i.then_inc(t_mm, 1)
                    if not is_last:
                        for u in SUB[k]:
                            scores(q + 1, u)
                    if k > 0:
                        weighted(q, par, k - 1)
                    elif not is_first:
                        weighted(q - 1, 1 - par, NSTEP - 1)
                    if not is_first and k == 5:
                        out_h(q - 1)
                    if not is_first and k == 8:
                        out_g(q - 1)
                    if not is_last and k == 13 and not (isinstance(q, int) and q + 2 >= NQ):
                        query(q + 2)

            query(0)
            for u in range(QB * NC):
                scores(0, u)
            query(1)
            pairs(pe, pair)
            weighted(NQ - 1, 1, NSTEP - 1)
            out_h(NQ - 1)
            out_g(NQ - 1)


INPUTS = ["beta", "L0_gnn_kernel", "L0_gnn_bias", "L1_gnn_W1", "L1_gnn_b1", "L1_gnn_W2", "L1_gnn_b2", "L1_gnn_W3",
          "L1_gnn_b3", "L2_gnn_W", "L2_gnn_b", "L3_gnn_W_l", "L3_gnn_W_r", "L3_gnn_W_h", "L3_gnn_W_g",
          "L3_gnn_gamma"]


def kernel(**inputs):
    import concourse.bacc as bacc
    from concourse.bass_utils import run_bass_kernel_spmd

    nc = bacc.Bacc("TRN2", target_bir_lowering=False, num_devices=1, dynamic_dma_scratch_size=4096)
    adj = np.asarray(inputs["adj"]).reshape(P, NC, CB, P, NB)
    streamed = adj[..., :NS * GB].reshape(P, NC, CB, P, NS, GB).transpose(1, 4, 3, 5, 2, 0)
    kept = adj[..., NS * GB:].transpose(1, 3, 4, 2, 0)
    arrays = {
        "adj_s": np.ascontiguousarray(streamed).reshape(NC * NS, P, TW),
        "adj_r": np.ascontiguousarray(kept).reshape(NC, P, RW),
        "x": np.ascontiguousarray(inputs["x"]).reshape(P, NB * D),
        "beta": np.ascontiguousarray(inputs["L0_gnn_beta"]).reshape(P, NB),
        "ident": np.eye(P, dtype=np.float32),
        "comb": np.concatenate([np.eye(H, P, dtype=np.float32)] * 2),
    }
    for name in INPUTS[1:]:
        arrays[name] = np.ascontiguousarray(inputs[name])
    aps = {k: nc.dram_tensor(f"in_{k}", a.shape, F32, kind="ExternalInput").ap() for k, a in arrays.items()}
    out = nc.dram_tensor("out", (P, NB * D), F32, kind="ExternalOutput").ap()
    build(nc, aps["adj_s"], aps["adj_r"], aps["x"], aps["beta"], aps["ident"], aps["comb"], aps, out)
    r = run_bass_kernel_spmd(nc, [{f"in_{k}": a for k, a in arrays.items()}], core_ids=[0])
    return np.asarray(r.results[0]["out"]).reshape(N, D)
```

```python
from contextlib import ExitStack

import numpy as np

import concourse.bass as bass
from concourse import mybir

F32 = mybir.dt.float32
F32R = mybir.dt.float32r
ALU = mybir.AluOpType
ACT = mybir.ActivationFunctionType
AX_X = mybir.AxisListType.X

P = 128
N = 4096
D = 128
H = 20
NB = N // P
CB = 4
CW = CB * P
NC = NB // CB
GB = 2
NG = NB // GB
RB = 4
NS = NG - RB // GB
TW = GB * CW
NSWEEP = 6
NARROW = (1, 2, 3)
FIRST_SUMMED = 0
ADDS = ((1, 1), (2, 2), (3, 3), (6, "res0"), (8, 8), (9, 9), (10, 10), (11, 11), (12, "res1"))
SUMMED = (FIRST_SUMMED,) + tuple(t for _, t in ADDS if isinstance(t, int))
NSUM = len(ADDS)
FIRST_ONES = min(g for g in range(NS) if g not in SUMMED)
KEPT_AFTER = (3, 6, 9, NS - 1)
RW = RB * CW
RAW = 8
HL = 4
XP = 4
EPS = 1e-5
LAST_HALF = (2, 3)
SQRT_GUARD = 1e-8
QB = 2
QW = QB * P
NQ = NB // QB
NSTEP = NB // 2
EQ = 4
EW = N // EQ

STAGES = {
    "xb": (0, 3, 4, 5), "bx": (0,), "xw": (0, 3, 4), "at": range(6), "rs": (0,), "sq": (0,),
    "h1": (1, 2), "dinv0": (0,), "deg": (0,), "inv": (0,), "dg2": (0,), "t1": (0, 3, 4),
    "resid": (0, 3, 4), "bst": (0, 3, 4), "agg": (0, 3, 4), "var": (0, 3, 4), "std": (0, 3, 4),
    "rc": (0, 3, 4), "rstd": (0, 3, 4), "norm": (0, 3, 4), "xt": (0, 3), "ht": (5,), "uw": (0, 1, 2),
    "vw": (3,), "xfin": (5,), "mm1": range(6), "rr": (0,), "mm2": (1, 2), "tx": (0, 3), "mu": (0, 3),
}


def done(stage, s, c):
    return c + (1 + NC * sum(q < s for q in STAGES[stage]))


def build(nc, adj_s, adj_r, x_dram, beta_in, ident_in, comb_in, w, out):
    with ExitStack() as ctx:
        def sb(name, shape, dt=F32, on=ctx):
            return on.enter_context(nc.sbuf_tensor(name, shape, dt))

        def bank(name):
            return ctx.enter_context(nc.psum_tensor(name, [P, CW], F32))

        ident = sb("ident", [P, P])
        comb = sb("comb", [2 * H, P])
        ones_f = sb("ones_f", [P, P])
        ones_r = sb("ones_r", [P, P], F32R)
        k0 = sb("k0", [P, D])
        w1 = sb("w1", [P, H])
        w2 = sb("w2", [H, H])
        w3 = sb("w3", [2 * H, D])
        w_l2 = sb("w_l2", [P, D])
        w_q, w_k, w_h, w_g = (sb(n, [P, D]) for n in ("w_q", "w_k", "w_h", "w_g"))
        bias0 = sb("bias0", [P, D])
        bias3, bias_l2 = sb("bias3", [1, D]), sb("bias_l2", [1, D])
        b1, b2 = sb("b1", [H, 1]), sb("b2", [H, 1])
        gamma = sb("gamma", [P, 1])
        beta = sb("beta", [P, NB])
        dinv = sb("dinv", [P, NB])
        rs_row = sb("rs_row", [1, CW])
        sq, deg, inv, dg2 = (sb(n, [P, CB]) for n in ("sq", "deg", "inv", "dg2"))
        stats = sb("stats", [P, CB, 6])
        mv = sb("mv", [P, CB, 2])
        ve, std, rstd, nmr = (sb(n, [P, CB]) for n in ("ve", "std", "rstd", "nmr"))
        mv_all = sb("mv_all", [P, NB * 2])

        x = sb("x", [P, NB * D])
        v = sb("v", [P, NB * D])
        st_hi = sb("st_hi", [P, NB * D], F32R)
        with ExitStack() as narrow:
            kept_part = sb("kept_part", [P, NC * CW], F32, narrow)
        st_lo = sb("st_lo", [P, NB * D], F32R)

        with ExitStack() as swp:
            resident = sb("resident", [P, NC * RW], F32, swp)
            raw = sb("raw", [P, RAW, TW], F32, swp)
            t_hi = sb("t_hi", [P, HL, TW], F32R, swp)
            t_lo = sb("t_lo", [P, HL, TW], F32R, swp)
            at = sb("at", [P, CW], F32, swp)
            xt = sb("xt", [P, CW], F32, swp)
            xb = sb("xb", [P, CW], F32, swp)
            xs = sb("xs", [P, CW], F32, swp)
            xn = sb("xn", [P, CW], F32, swp)
            bx = sb("bx", [P, CW], F32, swp)
            rsum = sb("rsum", [P, TW], F32, swp)

        with ExitStack() as att:
            pb = [sb(f"pb{i}", [P, QB, N], F32, att) for i in range(2)]
            k_hi = sb("k_hi", [P, N], F32R, att)
            k_lo = sb("k_lo", [P, N], F32R, att)
            q_hi = sb("q_hi", [P, 2, QW], F32R, att)
            q_lo = sb("q_lo", [P, 2, QW], F32R, att)
            p_hi = sb("p_hi", [P, 2, 2 * QW], F32R, att)
            p_lo = sb("p_lo", [P, 2, 2 * QW], F32R, att)
            bt = sb("bt", [P, QW], F32, att)
            ct = sb("ct", [P, QW], F32, att)
            o_s = sb("o_s", [P, QW], F32, att)
            mx = [sb(f"mx{i}", [P, QB * NC], F32, att) for i in range(2)]
            mxr = sb("mxr", [P, QB], F32, att)
            nm = [sb(f"nm{i}", [P, QB], F32, att) for i in range(2)]
            ls = [sb(f"ls{i}", [P, QB * EQ], F32, att) for i in range(2)]
            lsum, lrec, lg = (sb(n, [P, QB], F32, att) for n in ("lsum", "lrec", "lg"))
            stats_a = sb("stats_a", [P, QB, 6], F32, att)
            mv_a = sb("mv_a", [P, QB, 2], F32, att)
            ve_a, std_a, rstd_a, nmr_a = (sb(n, [P, NB], F32, att) for n in ("ve_a", "std_a", "rstd_a", "nmr_a"))

        acc = [bank("acc0"), bank("acc1")]
        rs = [bank("rs0"), bank("rs1")]
        e0, e1, e2, e3 = (bank(f"e{i}") for i in range(4))

        def sem(name):
            return ctx.enter_context(nc.semaphore(name))

        past_wait = sem("past_wait")
        const_in, memset_done, out_done = sem("const_in"), sem("memset_done"), sem("out_done")
        x_in = [sem(f"x_in{i}") for i in range(XP)]
        raw_in = [sem(f"raw_in{i}") for i in range(RAW)]
        res_in = sem("res_in")
        hi_done, lo_done, pe_tile, pe_acc, sum_done = sem("hi_done"), sem("lo_done"), sem("pe_tile"), sem("pe_acc"), sem("sum_done")
        st_hi_done, st_lo_done = sem("st_hi_done"), sem("st_lo_done")
        kept_done = sem("kept_done")
        S = {k: sem(f"s_{k}") for k in STAGES}
        (k_mm, k_hi_done, k_lo_done, q_mm, q_hi_done, q_lo_done, s_mm, s_copied, max_done, negmax,
         exped, t_mm, ph_done, pl_done, pv_mm, bt_done, oh_mm, ct_done, og_mm, lsum_done, lrec_done,
         lg_done, o1_done, o2_done, sa_done, ga_done, mva_done, fin_ve, fin_std, fin_rc, fin_nmr,
         fin_x, fin_xa) = (sem(n) for n in (
            "k_mm k_hi_done k_lo_done q_mm q_hi_done q_lo_done s_mm s_copied max_done negmax "
            "exped t_mm ph_done pl_done pv_mm bt_done oh_mm ct_done og_mm lsum_done lrec_done "
            "lg_done o1_done o2_done sa_done ga_done mva_done fin_ve fin_std fin_rc fin_nmr fin_x fin_xa").split())

        def cols(t, c, width=CW):
            return t[:, c * width:(c + 1) * width] if isinstance(c, int) else t[:, bass.ds(c * width, width)]

        def blocks(ap, n=CB):
            return ap.rearrange("p (b f) -> p b f", b=n)

        def spread(ap, n=CB, width=D):
            return ap.unsqueeze(2).broadcast_to([P, n, width])

        def over_blocks(ap, n=CB):
            return ap.unsqueeze(1).broadcast_to([P, n, D])

        def chunks(eng, step):
            for s in range(NSWEEP):
                step(s, 0, 0)
                step(s, 1, 1)
                with eng.Fori(0, (NC - 2) // 2) as i:
                    step(s, i * 2 + 2, 0)
                    step(s, i * 2 + 3, 1)

        def tile_blocks(s, g):
            return GB - 1 if s in LAST_HALF and g == NS - 1 else GB

        def first(c):
            return isinstance(c, int) and c == 0

        def before(s, c):
            return (s - 1, NC - 1) if first(c) else (s, c - 1)

        def tile_no(s, c, g):
            return c * NS + (NC * NS * s + g)

        def landed(s, c, g):
            per = (NS - 1 - g % RAW) // RAW + 1
            return c * (16 * per) + 16 * (per * NC * s + g // RAW + 1)

        def wait_slot(sp, s, c, g):
            if g >= RAW:
                qs, qc, qg = s, c, g - RAW
            else:
                qs, qc = before(s, c)
                qg = g + (NS - 1 - g) // RAW * RAW
            if qs == 0 and qg in SUMMED:
                n = [t for _, t in ADDS].index(qg or ADDS[0][1])
                sp.wait_ge(sum_done, qc * NSUM + (n + 1))
            else:
                sp.wait_ge(lo_done, tile_no(qs, qc, qg) + 1)
                if qs == LAST_HALF[0] - 1 and qg == NS - 1:
                    sp.wait_ge(kept_done, qc + 1)

        def group(t, g):
            return t[:, g * GB * D:(g + 1) * GB * D]

        def block_of(t, b):
            return t[:, b * D:(b + 1) * D]

        def pairs(eng, pair):
            pair(0, 0, True, False)
            pair(1, 1, False, False)
            with eng.Fori(0, (NQ - 4) // 2) as i:
                pair(i * 2 + 2, 0, False, False)
                pair(i * 2 + 3, 1, False, False)
            pair(NQ - 2, 0, False, False)
            pair(NQ - 1, 1, False, True)

        SUB = [[0, 1], [2], [3], [4], [5], [6], [7], [8, 9], [10], [11], [12], [13], [14], [15], [], []]
        EXP_OWN = {1: (1, 0), 2: (1, 1), 4: (2, 0), 6: (2, 1), 8: (3, 0), 10: (3, 1)}
        EXP_NEXT = {12: (0, 0), 14: (0, 1)}

        LN_PARTS = ((0, NB - 2 * QB), (NB - 2 * QB, NB))
        ACT_LN = {12: (0, 4), 13: (4, 8), 14: (8, 12), 15: (12, 16)}
        DVE_LN = {12: (16, 19), 13: (19, 22), 14: (22, 25), 15: (25, 28)}
        RESULT = ((0, 8, 1), (16, 22, 0), (8, 16, 1), (22, 28, 0), (28, 32, 0))

        consts = [(ident, ident_in), (comb, comb_in), (k0, w["L0_gnn_kernel"]), (w1, w["L1_gnn_W1"]),
                  (w2, w["L1_gnn_W2"]), (w3[0:H, :], w["L1_gnn_W3"]), (w3[H:2 * H, :], w["L1_gnn_W3"]),
                  (w_l2, w["L2_gnn_W"]), (w_q, w["L3_gnn_W_l"]), (w_k, w["L3_gnn_W_r"]),
                  (w_h, w["L3_gnn_W_h"]), (w_g, w["L3_gnn_W_g"]),
                  (b1, w["L1_gnn_b1"].rearrange("(h a) -> h a", a=1)),
                  (b2, w["L1_gnn_b2"].rearrange("(h a) -> h a", a=1)),
                  (bias0, w["L0_gnn_bias"].partition_broadcast(P)),
                  (bias3, w["L1_gnn_b3"].rearrange("(a f) -> a f", a=1)),
                  (bias_l2, w["L2_gnn_b"].rearrange("(a f) -> a f", a=1)),
                  (gamma, w["L3_gnn_gamma"].partition_broadcast(P)), (beta, beta_in)]
        n_const = 16 * len(consts)

        def kept_block(c):
            return cols(kept_part, c)

        def alone(eng):
            eng.sem_inc(past_wait, 1)

        def source(s):
            return x if s in (0, 5) else v

        def wait_source(eng, s, g):
            if s == 0:
                eng.wait_ge(x_in[g * XP // NG], 16)
            elif s in (1, 2, 3):
                eng.wait_ge(S["uw"], done("uw", s - 1, g * GB // CB))
            elif s == 4:
                eng.wait_ge(S["vw"], done("vw", 3, g * GB // CB))
            else:
                eng.wait_ge(S["xw"], done("xw", 4, g * GB // CB))

        block = ctx.enter_context(nc.Block())

        @block.sync
        def _(sp):
            def tile(c, g):
                return rows(adj_s, c * NS + g)

            def rows(t, n):
                return t[n] if isinstance(n, int) else t[bass.ds(n, 1)].rearrange("a p n -> (a p) n")

            def step(s, c, par):
                for g in range(NS):
                    if s == 0 and first(c):
                        if g % 2 == 0 and g < 2 * XP:
                            part = g // 2
                            sp.dma_start(cols(x, part, NB * D // XP),
                                         cols(x_dram, part, NB * D // XP)).then_inc(x_in[part], 16)
                        if g == 6:
                            for dst, src in consts:
                                sp.dma_start(dst[:, :], src).then_inc(const_in, 16)
                    if s == 0 and g == (7 if first(c) else 0):
                        if not first(c):
                            sp.wait_ge(res_in, c * 16)
                        sp.dma_start(cols(resident, c, RW), rows(adj_r, c)).then_inc(res_in, 16)
                    if not (s == 0 and first(c) and g < RAW):
                        wait_slot(sp, s, c, g)
                    n = tile_blocks(s, g) * CW
                    sp.dma_start(raw[:, g % RAW, :n], tile(c, g)[:, :n]).then_inc(raw_in[g % RAW], 16)

            chunks(sp, step)
            for n, (a, b, by_act) in enumerate(RESULT):
                if by_act:
                    sp.wait_ge(fin_xa, sum(r[2] for r in RESULT[:n]) + 1)
                else:
                    sp.wait_ge(fin_x, sum(not r[2] for r in RESULT[:n]) + 1)
                sp.dma_start(out[:, a * D:b * D], v[:, a * D:b * D]).then_inc(out_done, 16)
            sp.wait_ge(out_done, 16 * len(RESULT))

        @block.gpsimd
        def _(pool):
            nc.gpsimd.memset(v[:], 0.0).then_inc(memset_done, 1)
            pool.wait_ge(const_in, n_const)
            for part in x_in:
                pool.wait_ge(part, 16)

            def keep_old_x(s, c):
                if s == 5:
                    if first(c):
                        pool.wait_ge(S["resid"], done("resid", 4, NC - 1))
                    else:
                        pool.wait_ge(S["xfin"], done("xfin", 5, c) - 1)
                        pool.wait_ge(S["mm1"], done("mm1", 5, c) - 1)
                    pool.wait_ge(S["xw"], done("xw", 4, NC - 1))
                else:
                    if not (s == 0 and first(c)):
                        pool.wait_ge(S["resid"], done("resid", s, c) - 1)
                        pool.wait_ge(S["xw"], done("xw", s, c) - 1)
                alone(pool)
                if s == 0:
                    nc.gpsimd.tensor_tensor(blocks(xb[:, :]), blocks(cols(x, c)), over_blocks(bias0[:, :]),
                                            ALU.add).then_inc(S["xb"], 1)
                else:
                    nc.gpsimd.tensor_copy(xb[:, :], cols(x, c)).then_inc(S["xb"], 1)

            def step(s, c, par):
                has_before = not (s == 0 and first(c))
                ps, pc = before(s, c)
                if has_before and ps in STAGES["xb"]:
                    keep_old_x(ps, pc)
                if s == 0:
                    if not first(c):
                        pool.wait_ge(pe_acc, c)
                        alone(pool)
                    nc.gpsimd.tensor_tensor(blocks(bx[:, :]), blocks(cols(x, c)), spread(cols(beta, c, CB)),
                                            ALU.mult).then_inc(S["bx"], 1)
                if has_before and ps in STAGES["xw"]:
                    pool.wait_ge(S["norm"], done("norm", ps, pc))
                    alone(pool)
                    nc.gpsimd.tensor_copy(cols(x, pc), xn[:, :]).then_inc(S["xw"], 1)

            chunks(pool, step)
            keep_old_x(5, NC - 1)

        @block.scalar
        def _(act):

            def stationary_hi(s, g):
                if s > 0 and g < NS:
                    act.wait_ge(pe_tile, tile_no(s - 1, NC - 1, g) + 1)
                wait_source(act, s, g)
                nc.scalar.activation(group(st_hi, g), group(source(s), g), ACT.Copy).then_inc(st_hi_done, 1)

            def evacuate(s, c, par):
                act.wait_ge(pe_acc, c + (NC * s + 1))
                if not (s == 0 and first(c)):
                    act.wait_ge(S["mm1"], done("mm1", s, c) - 1)
                rows = slice(0, 2 * H if s in NARROW else P)
                nc.scalar.activation(at[rows, :], acc[par][rows, :], ACT.Copy).then_inc(S["at"], 1)
                if s == 0:
                    nc.scalar.activation(rs_row[:, :], rs[par][0:1, :], ACT.Copy).then_inc(S["rs"], 1)

            def second(s, c):
                if s == 0:
                    act.wait_ge(S["mm1"], done("mm1", s, c))
                    nc.scalar.activation(sq[:, :], e1[:, 0:CB], ACT.Sqrt).then_inc(S["sq"], 1)
                elif s in (1, 2):
                    act.wait_ge(S["mm1"], done("mm1", s, c))
                    nc.scalar.activation(xt[0:H, :], e2[0:H, :], ACT.Relu,
                                         bias=(b1 if s == 1 else b2)[:, 0:1]).then_inc(S["h1"], 1)
                elif s == 5:
                    act.wait_ge(S["mm1"], done("mm1", s, c))
                    nc.scalar.activation(cols(v, c), e2[:, :], ACT.Copy).then_inc(S["ht"], 1)

            def deviation(s, c):
                if s in STAGES["std"]:
                    act.wait_ge(S["var"], done("var", s, c))
                    nc.scalar.activation(std[:, :], ve[:, :], ACT.Sqrt).then_inc(S["std"], 1)

            def normalise(s, c):
                if s in STAGES["norm"]:
                    act.wait_ge(S["rstd"], done("rstd", s, c))
                    if not (s == 0 and first(c)):
                        act.wait_ge(S["xw"], done("xw", s, c) - 1)
                    for b in range(CB):
                        i = nc.scalar.activation(block_of(xn, b), block_of(xs, b), ACT.Identity,
                                                 bias=nmr[:, b:b + 1], scale=rstd[:, b:b + 1])
                    i.then_inc(S["norm"], 1)

            def transposed(s, c):
                if s in STAGES["xt"]:
                    act.wait_ge(S["tx"], done("tx", s, c))
                    if not (s == 0 and first(c)):
                        act.wait_ge(S["mu"], done("mu", s, c) - 1)
                    nc.scalar.activation(xt[:, :], e2[:, :], ACT.Copy).then_inc(S["xt"], 1)

            def next_h(s, c):
                if s in STAGES["uw"]:
                    if s == 0:
                        act.wait_ge(S["mu"], done("mu", s, c))
                        if first(c):
                            act.wait_ge(memset_done, 1)
                    else:
                        act.wait_ge(S["mm2"], done("mm2", s, c))
                    nc.scalar.activation(blocks(cols(v, c))[:, :, 0:H],
                                         e3[:, 0:CB * H].rearrange("p (b h) -> p b h", b=CB),
                                         ACT.Copy).then_inc(S["uw"], 1)

            def step(s, c, par):
                has_before = not (s == 0 and first(c))
                ps, pc = before(s, c)
                for g in range(NS):
                    if first(c):
                        stationary_hi(s, g)
                    act.wait_ge(raw_in[g % RAW], landed(s, c, g))
                    if not (s == 0 and first(c) and g < HL):
                        act.wait_ge(pe_tile, tile_no(s, c, g) - (HL - 1))
                    n = tile_blocks(s, g) * CW
                    nc.scalar.activation(t_hi[:, (par * NS + g) % HL, :n], raw[:, g % RAW, :n],
                                         ACT.Copy).then_inc(hi_done, 1)
                    if s == LAST_HALF[0] - 1 and g == NS - 1:
                        nc.scalar.activation(kept_block(c), raw[:, g % RAW, CW:], ACT.Copy).then_inc(kept_done, 1)
                    if has_before:
                        if g == 2:
                            evacuate(ps, pc, 1 - par)
                        if g == 4:
                            second(ps, pc)
                        if g == 8:
                            deviation(ps, pc)
                        if g == 10:
                            normalise(ps, pc)
                        if g == 12:
                            transposed(ps, pc)
                if has_before:
                    next_h(ps, pc)

            chunks(act, step)
            for g in range(NS, NG):
                stationary_hi(5, g)
            evacuate(5, NC - 1, 1)
            second(5, NC - 1)

            def keys_hi(c):
                act.wait_ge(k_mm, c + 1)
                nc.scalar.activation(cols(k_hi, c), (acc[0], e3)[c % 2][:, :], ACT.Copy).then_inc(k_hi_done, 1)

            def query_hi(q, par):
                act.wait_ge(q_mm, q + 1)
                nc.scalar.activation(q_hi[:, par, :], e0[:, QW:2 * QW], ACT.Copy).then_inc(q_hi_done, 1)

            def exponent(q, par, j, rb):
                if j == 0 and rb == 0 and not (isinstance(q, int) and q < 2):
                    act.wait_ge(lsum_done, q - 1)
                if j == 0:
                    act.wait_ge(negmax, q * QB + (rb + 1))
                part = pb[par][:, rb, j * EW:(j + 1) * EW]
                nc.scalar.activation(part, part, ACT.Exp, bias=nm[par][:, rb:rb + 1],
                                     accum_out=ls[par][:, rb * EQ + j:rb * EQ + j + 1]).then_inc(exped, 1)

            def pair(q, par, is_first, is_last):
                for k in range(NSTEP):
                    act.wait_ge(t_mm, q * NSTEP + (k + 1))
                    if not (is_first and k < 2):
                        act.wait_ge(pv_mm, q * NSTEP + (k - 1))
                    nc.scalar.activation(p_hi[:, k % 2, :], (e2, e3)[k % 2][:, :], ACT.Copy).then_inc(ph_done, 1)
                    if k in EXP_OWN:
                        exponent(q, par, *EXP_OWN[k])
                    if not is_last and k in EXP_NEXT:
                        exponent(q + 1, 1 - par, *EXP_NEXT[k])
                    if is_last and k == 11:
                        last_deviation(0)
                    if is_last and k in ACT_LN:
                        last_norm(k)
                    if not is_first and k == 3:
                        act.wait_ge(pv_mm, q * NSTEP)
                        if not (isinstance(q, int) and q < 2):
                            act.wait_ge(oh_mm, q - 1)
                        nc.scalar.activation(bt[:, :], acc[1 - par][:, 0:QW], ACT.Copy).then_inc(bt_done, 1)
                    if not is_first and k == 7:
                        act.wait_ge(oh_mm, q)
                        nc.scalar.activation(ct[:, :], e0[:, 0:QW], ACT.Copy).then_inc(ct_done, 1)
                    if not is_last and k == 11 and not (isinstance(q, int) and q + 2 >= NQ):
                        query_hi(q + 2, par)

            def last_deviation(part):
                a, b = LN_PARTS[part]
                act.wait_ge(fin_ve, part + 1)
                nc.scalar.activation(std_a[:, a:b], ve_a[:, a:b], ACT.Sqrt).then_inc(fin_std, 1)

            def last_norm(k):
                a, b = ACT_LN[k]
                act.wait_ge(fin_nmr, 1)
                for n in range(a, b):
                    i = nc.scalar.activation(block_of(v, n), block_of(x, n), ACT.Identity,
                                             bias=nmr_a[:, n:n + 1], scale=rstd_a[:, n:n + 1])
                if b in [r[1] for r in RESULT]:
                    i.then_inc(fin_xa, 1)

            for c in range(NC):
                keys_hi(c)
                if c in (2, 4):
                    query_hi(c // 2 - 1, c // 2 - 1)
            exponent(0, 0, 0, 0)
            exponent(0, 0, 0, 1)
            pairs(act, pair)
            act.wait_ge(pv_mm, NQ * NSTEP)
            act.wait_ge(oh_mm, NQ - 1)
            nc.scalar.activation(bt[:, :], acc[1][:, 0:QW], ACT.Copy).then_inc(bt_done, 1)
            act.wait_ge(oh_mm, NQ)
            nc.scalar.activation(ct[:, :], e0[:, 0:QW], ACT.Copy).then_inc(ct_done, 1)
            last_deviation(1)

        @block.vector
        def _(dve):
            nc.vector.memset(ones_f[:, :], 1.0).then_inc(memset_done, 1)
            nc.vector.memset(ones_r[:, :].bitcast(F32), 1.0).then_inc(memset_done, 1)

            def row_sum(c, n):
                if n == 0:
                    if not first(c):
                        dve.wait_ge(S["rr"], done("rr", 0, c) - 1)
                        dve.wait_ge(pe_acc, c)
                    nc.vector.tensor_tensor(rsum[:, :], raw[:, 0, :], raw[:, 1, :], ALU.add).then_inc(sum_done, 1)
                else:
                    dve.wait_ge(sum_done, c * NSUM + n)
                    tile = ADDS[n][1]
                    if isinstance(tile, int):
                        other = raw[:, tile % RAW, :]
                    else:
                        if tile == "res0":
                            dve.wait_ge(res_in, c * 16 + 16)
                        other = cols(resident, c * (RB // GB) + int(tile[3]), TW)
                    nc.vector.tensor_tensor(rsum[:, :], rsum[:, :], other, ALU.add).then_inc(sum_done, 1)

            def fold(c):
                dve.wait_ge(sum_done, c * NSUM + NSUM)
                nc.vector.tensor_tensor(rsum[:, 0:CW], rsum[:, 0:CW], rsum[:, CW:2 * CW],
                                        ALU.add).then_inc(S["rr"], 1)

            def stationary_lo(s, g, n):
                dve.wait_ge(st_hi_done, n + 1)
                if s in NARROW:
                    hi, src = blocks(group(st_hi, g)), blocks(group(v, g))
                    nc.vector.tensor_tensor(hi[:, :, H:2 * H], src[:, :, 0:H], hi[:, :, 0:H].bitcast(F32),
                                            ALU.subtract).then_inc(st_lo_done, 1)
                else:
                    nc.vector.tensor_tensor(group(st_lo, g), group(source(s), g), group(st_hi, g).bitcast(F32),
                                            ALU.subtract).then_inc(st_lo_done, 1)

            def degrees(s, c):
                if first(c):
                    dve.wait_ge(const_in, n_const)
                dve.wait_ge(S["sq"], done("sq", s, c))
                nc.vector.tensor_tensor(deg[:, :], e1[:, 0:CB], cols(beta, c, CB), ALU.add).then_inc(S["deg"], 1)
                nc.vector.tensor_scalar(dg2[:, :], sq[:, :], SQRT_GUARD, None, ALU.add).then_inc(S["dg2"], 1)
                dve.wait_ge(S["deg"], done("deg", s, c))
                nc.vector.reciprocal(inv[:, :], deg[:, :]).then_inc(S["inv"], 1)
                dve.wait_ge(S["dg2"], done("dg2", s, c))
                nc.vector.reciprocal(cols(dinv, c, CB), dg2[:, :]).then_inc(S["dinv0"], 1)

            def residual_1(s, c):
                if s in STAGES["resid"]:
                    dve.wait_ge(S["mm1"], done("mm1", s, c))
                    if not (s == 0 and first(c)):
                        dve.wait_ge(S["norm"], done("norm", s, c) - 1)
                    if s == 0:
                        degrees(s, c)
                        dve.wait_ge(S["inv"], done("inv", s, c))
                        nc.vector.tensor_tensor(blocks(xs[:, :]), blocks(e0[:, :]), spread(inv[:, :]),
                                                ALU.mult).then_inc(S["t1"], 1)
                    elif s == 3:
                        dve.wait_ge(S["xb"], done("xb", s, c))
                        nc.vector.scalar_tensor_tensor(out=xs[:, :], in0=e0[:, :], scalar=0.0, in1=xb[:, :],
                                                       op0=ALU.max, op1=ALU.add).then_inc(S["t1"], 1)
                    else:
                        nc.vector.tensor_tensor(blocks(xs[:, :]), blocks(e0[:, :]), spread(cols(dinv, c, CB)),
                                                ALU.mult).then_inc(S["t1"], 1)

            def residual_2(s, c):
                if s in STAGES["resid"]:
                    dve.wait_ge(S["t1"], done("t1", s, c))
                    if s == 3:
                        nc.vector.scalar_tensor_tensor(out=xs[:, :], in0=xs[:, :], scalar=0.0, in1=xb[:, :],
                                                       op0=ALU.max, op1=ALU.add).then_inc(S["resid"], 1)
                    else:
                        dve.wait_ge(S["xb"], done("xb", s, c))
                        nc.vector.tensor_tensor(xs[:, :], xs[:, :], xb[:, :], ALU.add).then_inc(S["resid"], 1)
                elif s == 5:
                    dve.wait_ge(S["mm1"], done("mm1", s, c))
                    dve.wait_ge(S["xb"], done("xb", s, c))
                    nc.vector.tensor_tensor(cols(x, c), e0[:, :], xb[:, :], ALU.add).then_inc(S["xfin"], 1)

            def statistics(s, c):
                if s in STAGES["bst"]:
                    dve.wait_ge(S["resid"], done("resid", s, c))
                    for b in range(CB):
                        i = nc.vector.bn_stats(stats[:, b, :], block_of(xs, b))
                    i.then_inc(S["bst"], 1)
                    dve.wait_ge(S["bst"], done("bst", s, c))
                    alone(dve)
                    for b in range(CB):
                        i = nc.vector.bn_aggr(mv[:, b, :], stats[:, b, :])
                    i.then_inc(S["agg"], 1)
                    dve.wait_ge(S["agg"], done("agg", s, c))
                    nc.vector.tensor_scalar(ve[:, :], mv[:, :, 1], EPS, None, ALU.add).then_inc(S["var"], 1)

            def scales(s, c):
                if s in STAGES["rc"]:
                    dve.wait_ge(S["std"], done("std", s, c))
                    nc.vector.reciprocal(rstd[:, :], std[:, :]).then_inc(S["rc"], 1)
                    dve.wait_ge(S["rc"], done("rc", s, c))
                    nc.vector.scalar_tensor_tensor(out=nmr[:, :], in0=mv[:, :, 0], scalar=-1.0, in1=rstd[:, :],
                                                   op0=ALU.mult, op1=ALU.mult).then_inc(S["rstd"], 1)

            def laplacian_h(c):
                dve.wait_ge(S["mu"], done("mu", 3, c))
                nc.vector.tensor_tensor(blocks(cols(v, c)), blocks(e3[:, :]), spread(cols(dinv, c, CB)),
                                        ALU.mult).then_inc(S["vw"], 1)

            def step(s, c, par):
                has_before = not (s == 0 and first(c))
                ps, pc = before(s, c)
                for g in range(NS):
                    if first(c):
                        stationary_lo(s, g, NS * s + g)
                    dve.wait_ge(hi_done, tile_no(s, c, g) + 1)
                    n = tile_blocks(s, g) * CW
                    nc.vector.tensor_tensor(t_lo[:, (par * NS + g) % HL, :n], raw[:, g % RAW, :n],
                                            t_hi[:, (par * NS + g) % HL, :n].bitcast(F32),
                                            ALU.subtract).then_inc(lo_done, 1)
                    for n, (after, _) in enumerate(ADDS):
                        if s == 0 and after == g:
                            row_sum(c, n)
                    if g == 1:
                        if s == 3 and not (isinstance(c, int) and c < 2):
                            laplacian_h(c - 2)
                        if s == 4 and first(c):
                            laplacian_h(NC - 2)
                    if has_before:
                        if g == 4:
                            residual_1(ps, pc)
                        if g == 5:
                            residual_2(ps, pc)
                        if g == 6:
                            statistics(ps, pc)
                        if g == 8:
                            scales(ps, pc)
                if s == 0:
                    fold(c)
                if s == 4 and first(c):
                    laplacian_h(NC - 1)

            chunks(dve, step)
            for g in range(NS, NG):
                stationary_lo(5, g, NSWEEP * NS + g - NS)
            dve.wait_ge(st_lo_done, NSWEEP * NS + NG - NS)
            residual_2(5, NC - 1)

            def keys_lo(c):
                dve.wait_ge(k_hi_done, c + 1)
                nc.vector.tensor_tensor(cols(k_lo, c), (acc[0], e3)[c % 2][:, :], cols(k_hi, c).bitcast(F32),
                                        ALU.subtract).then_inc(k_lo_done, 1)

            def query_lo(q, par):
                dve.wait_ge(q_hi_done, q + 1)
                nc.vector.tensor_tensor(q_lo[:, par, :], e0[:, QW:2 * QW], q_hi[:, par, :].bitcast(F32),
                                        ALU.subtract).then_inc(q_lo_done, 1)

            def scores(q, par, u):
                rb, j = divmod(u, NC)
                dve.wait_ge(s_mm, q * (QB * NC) + (u + 1))
                nc.vector.tensor_scalar(pb[par][:, rb, j * CW:(j + 1) * CW], rs[u % 2][:, :], 1.0, None, ALU.mult,
                                        ALU.max, accum_out=mx[par][:, u:u + 1]).then_inc(s_copied, 1)
                if j == NC - 1:
                    dve.wait_ge(s_copied, q * (QB * NC) + (u + 1))
                    nc.vector.reduce_max(mxr[:, rb:rb + 1], mx[par][:, rb * NC:(rb + 1) * NC],
                                         AX_X).then_inc(max_done, 1)
                    dve.wait_ge(max_done, q * QB + (rb + 1))
                    nc.vector.tensor_scalar(nm[par][:, rb:rb + 1], mxr[:, rb:rb + 1], -1.0, None,
                                            ALU.mult).then_inc(negmax, 1)

            def finish_sums(q, par):
                dve.wait_ge(exped, (q + 1) * (QB * EQ))
                nc.vector.reduce_sum(lsum[:, :], ls[par][:, :].rearrange("p (b j) -> p b j", b=QB),
                                     AX_X).then_inc(lsum_done, 1)
                dve.wait_ge(lsum_done, q + 1)
                nc.vector.reciprocal(lrec[:, :], lsum[:, :]).then_inc(lrec_done, 1)
                dve.wait_ge(lrec_done, q + 1)
                nc.vector.tensor_scalar(lg[:, :], lrec[:, :], gamma[:, 0:1], None, ALU.mult).then_inc(lg_done, 1)

            def finish_add(q):
                dve.wait_ge(lg_done, q + 1)
                dve.wait_ge(og_mm, q + 1)
                nc.vector.tensor_tensor(blocks(o_s[:, :], QB), blocks(e1[:, 0:QW], QB), spread(lg[:, :], QB),
                                        ALU.mult).then_inc(o1_done, 1)
                dve.wait_ge(o1_done, q + 1)
                nc.vector.tensor_tensor(cols(x, q, QW), o_s[:, :], cols(x, q, QW), ALU.add).then_inc(o2_done, 1)

            def finish_stats(q):
                dve.wait_ge(o2_done, q + 1)
                for b in range(QB):
                    i = nc.vector.bn_stats(stats_a[:, b, :], cols(x, q * QB + b, D))
                i.then_inc(sa_done, 1)
                dve.wait_ge(sa_done, q + 1)
                alone(dve)
                for b in range(QB):
                    i = nc.vector.bn_aggr(mv_a[:, b, :], stats_a[:, b, :])
                i.then_inc(ga_done, 1)
                dve.wait_ge(ga_done, q + 1)
                nc.vector.tensor_copy(cols(mv_all, q, 2 * QB), mv_a[:, :, :].rearrange("p b t -> p (b t)")).then_inc(
                    mva_done, 1)

            def pair(q, par, is_first, is_last):
                for k in range(NSTEP):
                    dve.wait_ge(ph_done, q * NSTEP + (k + 1))
                    nc.vector.tensor_tensor(p_lo[:, k % 2, :], (e2, e3)[k % 2][:, :],
                                            p_hi[:, k % 2, :].bitcast(F32), ALU.subtract).then_inc(pl_done, 1)
                    if not is_last:
                        for u in SUB[k]:
                            scores(q + 1, 1 - par, u)
                    if is_last and k == 9:
                        last_variance(0)
                    if is_last and k == 11:
                        last_scales(0)
                    if is_last and k in DVE_LN:
                        last_norm(*DVE_LN[k])
                    if not is_first and k == 2:
                        finish_sums(q - 1, 1 - par)
                    if not is_first and k == 10:
                        finish_add(q - 1)
                    if not is_first and k == 12:
                        finish_stats(q - 1)
                    if not is_last and k == 11 and not (isinstance(q, int) and q + 2 >= NQ):
                        query_lo(q + 2, par)

            mva = mv_all[:, :].rearrange("p (b t) -> p b t", t=2)

            def last_variance(part):
                a, b = LN_PARTS[part]
                dve.wait_ge(mva_done, b // QB)
                nc.vector.tensor_scalar(ve_a[:, a:b], mva[:, a:b, 1], EPS, None, ALU.add).then_inc(fin_ve, 1)

            def last_scales(part):
                a, b = LN_PARTS[part]
                dve.wait_ge(fin_std, part + 1)
                nc.vector.reciprocal(rstd_a[:, a:b], std_a[:, a:b]).then_inc(fin_rc, 1)
                dve.wait_ge(fin_rc, part + 1)
                nc.vector.scalar_tensor_tensor(out=nmr_a[:, a:b], in0=mva[:, a:b, 0], scalar=-1.0,
                                               in1=rstd_a[:, a:b], op0=ALU.mult, op1=ALU.mult).then_inc(fin_nmr, 1)
                dve.wait_ge(fin_nmr, part + 1)

            def last_norm(a, b):
                for n in range(a, b):
                    i = nc.vector.tensor_scalar(block_of(v, n), block_of(x, n), rstd_a[:, n:n + 1],
                                                nmr_a[:, n:n + 1], ALU.mult, ALU.add)
                if b in [r[1] for r in RESULT]:
                    i.then_inc(fin_x, 1)

            for c in range(NC):
                keys_lo(c)
                if c in (2, 4):
                    query_lo(c // 2 - 1, c // 2 - 1)
                if c > 2:
                    scores(0, 0, c - 3)
            for u in range(NC - 3, QB * NC):
                scores(0, 0, u)
            pairs(dve, pair)
            finish_sums(NQ - 1, 1)
            finish_add(NQ - 1)
            finish_stats(NQ - 1)
            last_variance(1)
            last_scales(1)
            last_norm(*LN_PARTS[1])

        @block.tensor
        def _(pe):
            pe.wait_ge(memset_done, 3)
            mm = nc.tensor.matmul

            def epilogue_1(s, c, par):
                pe.wait_ge(S["at"], done("at", s, c))
                if s == 0:
                    pe.wait_ge(S["rs"], done("rs", s, c))
                    for b in range(CB):
                        mm(e0[:, b * D:(b + 1) * D], block_of(at, b), k0[:, :], start=True, stop=True)
                    for b in range(CB):
                        i = mm(e1[:, b:b + 1], rs_row[0:1, b * P:(b + 1) * P], ones_f[0:1, 0:1],
                               start=True, stop=True)
                elif s in (1, 2):
                    i = mm(e2[:, :], comb[:, :], at[0:2 * H, :], start=True, stop=True)
                elif s == 3:
                    for b in range(CB):
                        mm(e0[:, b * D:(b + 1) * D], ones_f[0:1, :], bias3[:, :], start=True, stop=False)
                        i = mm(e0[:, b * D:(b + 1) * D], at[0:2 * H, b * P:(b + 1) * P], w3[:, :],
                               start=False, stop=True)
                else:
                    if s == 4:
                        pe.wait_ge(S["t1"], done("t1", 4, c) - 1)
                    elif first(c):
                        pe.wait_ge(S["t1"], done("t1", 4, NC - 1))
                    else:
                        pe.wait_ge(S["xfin"], done("xfin", 5, c) - 1)
                    for b in range(CB):
                        i = mm(e0[:, b * D:(b + 1) * D], block_of(at, b), ident[:, :], is_transpose=True,
                               start=True, stop=True)
                    if s == 5:
                        if not first(c):
                            pe.wait_ge(S["ht"], done("ht", 5, c) - 1)
                        pe.wait_ge(S["xb"], done("xb", 5, c))
                        for b in range(CB):
                            i = mm(e2[:, b * D:(b + 1) * D], block_of(xb, b), ident[:, :], is_transpose=True,
                                   start=True, stop=True)
                i.then_inc(S["mm1"], 1)

            def epilogue_2(s, c):
                if s in (1, 2):
                    pe.wait_ge(S["h1"], done("h1", s, c))
                    pe.wait_ge(S["uw"], done("uw", s, c) - 1)
                    for b in range(CB):
                        i = mm(e3[:, b * H:(b + 1) * H], xt[0:H, b * P:(b + 1) * P],
                               w2[:, :] if s == 1 else ident[0:H, 0:H], start=True, stop=True)
                    i.then_inc(S["mm2"], 1)

            def epilogue_3(s, c):
                if s in (0, 3):
                    pe.wait_ge(S["norm"], done("norm", s, c))
                    for b in range(CB):
                        i = mm(e2[:, b * D:(b + 1) * D], block_of(xn, b), ident[:, :], is_transpose=True,
                               start=True, stop=True)
                    i.then_inc(S["tx"], 1)

            def epilogue_4(s, c):
                if s in (0, 3):
                    pe.wait_ge(S["xt"], done("xt", s, c))
                    if s == 0 and not first(c):
                        pe.wait_ge(S["uw"], done("uw", 0, c) - 1)
                    if s == 3:
                        if first(c):
                            pe.wait_ge(S["uw"], done("uw", 2, NC - 1))
                        else:
                            pe.wait_ge(S["vw"], done("vw", 3, c) - 1)
                    wide, rhs = (H, w1) if s == 0 else (D, w_l2)
                    for b in range(CB):
                        if s == 3:
                            mm(e3[:, b * D:(b + 1) * D], ones_f[0:1, :], bias_l2[:, :], start=True, stop=False)
                        i = mm(e3[:, b * wide:(b + 1) * wide], block_of(xt, b), rhs[:, :], start=(s == 0), stop=True)
                    i.then_inc(S["mu"], 1)

            def step(s, c, par):
                has_before = not (s == 0 and first(c))
                ps, pc = before(s, c)
                a, r = acc[par], rs[par]
                if not (s == 0 and isinstance(c, int) and c < 2):
                    pe.wait_ge(S["at"], done("at", s, c) - 2)
                    if s == 0:
                        pe.wait_ge(S["rs"], done("rs", s, c) - 2)
                for g in range(NS):
                    hi, lo = t_hi[:, (par * NS + g) % HL, :], t_lo[:, (par * NS + g) % HL, :]
                    ones_too = s == 0 and g not in SUMMED
                    if first(c):
                        pe.wait_ge(st_lo_done, NS * s + g + 1)
                    pe.wait_ge(hi_done, tile_no(s, c, g) + 1)
                    for j in range(tile_blocks(s, g)):
                        b, m = g * GB + j, slice(j * CW, (j + 1) * CW)
                        mm(a[:, :], block_of(st_hi, b), hi[:, m], start=(b == 0), stop=False)
                        if s not in NARROW:
                            mm(a[:, :], block_of(st_lo, b), hi[:, m], start=False, stop=False)
                        if ones_too:
                            mm(r[:, :], ones_r[:, :], hi[:, m], start=(g == FIRST_ONES and j == 0), stop=False)
                    pe.wait_ge(lo_done, tile_no(s, c, g) + 1)
                    for j in range(tile_blocks(s, g)):
                        b, m = g * GB + j, slice(j * CW, (j + 1) * CW)
                        if ones_too:
                            mm(r[:, :], ones_r[:, :], lo[:, m], start=False, stop=False)
                        i = mm(a[:, :], block_of(st_hi, b), lo[:, m], start=False, stop=False)
                    i.then_inc(pe_tile, 1)
                    if has_before:
                        if g == 1:
                            epilogue_1(ps, pc, 1 - par)
                        if g == 5:
                            epilogue_2(ps, pc)
                        if g == 9:
                            epilogue_3(ps, pc)
                        if g == 11:
                            epilogue_4(ps, pc)
                    if s == 0 and g == 4:
                        if first(c):
                            pe.wait_ge(const_in, n_const)
                        pe.wait_ge(S["bx"], done("bx", 0, c))
                        for b in range(CB):
                            mm(a[:, b * D:(b + 1) * D], block_of(bx, b), ident[:, :], start=False, stop=False)
                    if s == 0 and g == NS - 1:
                        pe.wait_ge(S["rr"], done("rr", 0, c))
                        mm(r[:, :], ones_f[:, :], rsum[:, 0:CW], start=False, stop=True)
                    if g in KEPT_AFTER and not first(c):
                        kept = [KEPT_AFTER.index(g)]
                    elif g == NS - 1:
                        kept = range(RB)
                        wait_source(pe, s, NG - 1)
                    else:
                        kept = []
                    if tile_blocks(s, g) < GB:
                        if s == LAST_HALF[0]:
                            pe.wait_ge(kept_done, c + 1)
                        mm(a[:, :], block_of(st_hi, NS * GB - 1).bitcast(F32), kept_block(c), start=False, stop=False)
                    if s == 0 and len(kept) and kept[0] == 0:
                        pe.wait_ge(res_in, c * 16 + 16)
                    for j in kept:
                        i = mm(a[:, :], block_of(source(s), NS * GB + j), cols(resident, c * RB + j),
                               start=False, stop=(j == RB - 1))
                    if g == NS - 1:
                        i.then_inc(pe_acc, 1)

            chunks(pe, step)

            def keys(c):
                pe.wait_ge(S["ht"], done("ht", 5, c))
                if c == 0:
                    pe.wait_ge(S["at"], done("at", 5, NC - 2))
                elif c > 1:
                    pe.wait_ge(k_lo_done, c - 1)
                mm((acc[0], e3)[c % 2][:, :], w_k[:, :], cols(v, c), start=True, stop=True).then_inc(k_mm, 1)

            def query(q):
                if isinstance(q, int) and q == 0:
                    pe.wait_ge(S["xfin"], done("xfin", 5, NC - 1))
                elif isinstance(q, int) and q == 1:
                    pe.wait_ge(q_lo_done, 1)
                elif not (isinstance(q, int) and q == 2):
                    pe.wait_ge(ct_done, q - 2)
                mm(e0[:, QW:2 * QW], w_q[:, :], cols(v, q, QW), start=True, stop=True).then_inc(q_mm, 1)

            def scores(q, par, u):
                rb, j = divmod(u, NC)
                if u == 0:
                    pe.wait_ge(q_lo_done, q + 1)
                if not (isinstance(q, int) and q == 0 and u < 2):
                    pe.wait_ge(s_copied, q * (QB * NC) + (u - 1))
                if isinstance(q, int) and q == 0:
                    pe.wait_ge(k_lo_done, j + 1)
                qh, ql = block_of(q_hi[:, par, :], rb), block_of(q_lo[:, par, :], rb)
                kh, kl = cols(k_hi, j), cols(k_lo, j)
                mm(rs[u % 2][:, :], qh, kh, start=True, stop=False)
                mm(rs[u % 2][:, :], qh, kl, start=False, stop=False)
                mm(rs[u % 2][:, :], ql, kh, start=False, stop=True).then_inc(s_mm, 1)

            def weighted(q, par, k):
                pe.wait_ge(pl_done, q * NSTEP + (k + 1))
                if k == 0 and not (isinstance(q, int) and q < 2):
                    pe.wait_ge(bt_done, q - 1)
                o = acc[par][:, 0:QW]
                for u in range(2):
                    b = 2 * k + u
                    ph, pl = p_hi[:, k % 2, u * QW:(u + 1) * QW], p_lo[:, k % 2, u * QW:(u + 1) * QW]
                    mm(o, block_of(st_hi, b), ph, start=(b == 0), stop=False)
                    mm(o, block_of(st_hi, b), pl, start=False, stop=False)
                    i = mm(o, block_of(st_lo, b), ph, start=False, stop=(b == NB - 1))
                i.then_inc(pv_mm, 1)

            def out_h(q):
                pe.wait_ge(bt_done, q + 1)
                mm(e0[:, 0:QW], w_h[:, :], bt[:, :], start=True, stop=True).then_inc(oh_mm, 1)

            def out_g(q):
                pe.wait_ge(ct_done, q + 1)
                if not (isinstance(q, int) and q == 0):
                    pe.wait_ge(o1_done, q)
                for b in range(QB):
                    i = mm(e1[:, b * D:(b + 1) * D], block_of(ct, b), w_g[:, :], start=True, stop=True)
                i.then_inc(og_mm, 1)

            def pair(q, par, is_first, is_last):
                for k in range(NSTEP):
                    if k % 4 == 0:
                        pe.wait_ge(exped, q * (QB * EQ) + QB * (k // EQ + 1))
                    if not (is_first and k < 2):
                        pe.wait_ge(pl_done, q * NSTEP + (k - 1))
                    e = (e2, e3)[k % 2]
                    for u in range(2):
                        for rb in range(QB):
                            col = (2 * k + u) * P
                            i = mm(e[:, u * QW + rb * P:u * QW + (rb + 1) * P], pb[par][:, rb, col:col + P],
                                   ident[:, :], is_transpose=True, start=True, stop=True)
                    i.then_inc(t_mm, 1)
                    if not is_last:
                        for u in SUB[k]:
                            scores(q + 1, 1 - par, u)
                    if k > 0:
                        weighted(q, par, k - 1)
                    elif not is_first:
                        weighted(q - 1, 1 - par, NSTEP - 1)
                    if not is_first and k == 5:
                        out_h(q - 1)
                    if not is_first and k == 8:
                        out_g(q - 1)
                    if not is_last and k == 10 and not (isinstance(q, int) and q + 2 >= NQ):
                        query(q + 2)

            for c in range(NC):
                keys(c)
                if c == 1:
                    epilogue_1(5, NC - 1, 1)
                if c in (2, 4):
                    query(c // 2 - 1)
                if c > 2:
                    scores(0, 0, c - 3)
            for u in range(NC - 3, QB * NC):
                scores(0, 0, u)
            pe.wait_ge(st_lo_done, NSWEEP * NS + NG - NS)
            pairs(pe, pair)
            weighted(NQ - 1, 1, NSTEP - 1)
            out_h(NQ - 1)
            out_g(NQ - 1)


INPUTS = ["beta", "L0_gnn_kernel", "L0_gnn_bias", "L1_gnn_W1", "L1_gnn_b1", "L1_gnn_W2", "L1_gnn_b2", "L1_gnn_W3",
          "L1_gnn_b3", "L2_gnn_W", "L2_gnn_b", "L3_gnn_W_l", "L3_gnn_W_r", "L3_gnn_W_h", "L3_gnn_W_g",
          "L3_gnn_gamma"]


def kernel(**inputs):
    import concourse.bacc as bacc
    from concourse.bass_utils import run_bass_kernel_spmd

    nc = bacc.Bacc("TRN2", target_bir_lowering=False, num_devices=1, dynamic_dma_scratch_size=4096)
    adj = np.asarray(inputs["adj"]).reshape(P, NC, CB, P, NB)
    streamed = adj[..., :NS * GB].reshape(P, NC, CB, P, NS, GB).transpose(1, 4, 3, 5, 2, 0)
    kept = adj[..., NS * GB:].transpose(1, 3, 4, 2, 0)
    arrays = {
        "adj_s": np.ascontiguousarray(streamed).reshape(NC * NS, P, TW),
        "adj_r": np.ascontiguousarray(kept).reshape(NC, P, RW),
        "x": np.ascontiguousarray(inputs["x"]).reshape(P, NB * D),
        "beta": np.ascontiguousarray(inputs["L0_gnn_beta"]).reshape(P, NB),
        "ident": np.eye(P, dtype=np.float32),
        "comb": np.concatenate([np.eye(H, P, dtype=np.float32)] * 2),
    }
    for name in INPUTS[1:]:
        arrays[name] = np.ascontiguousarray(inputs[name])
    aps = {k: nc.dram_tensor(f"in_{k}", a.shape, F32, kind="ExternalInput").ap() for k, a in arrays.items()}
    out = nc.dram_tensor("out", (P, NB * D), F32, kind="ExternalOutput").ap()
    build(nc, aps["adj_s"], aps["adj_r"], aps["x"], aps["beta"], aps["ident"], aps["comb"], aps, out)
    r = run_bass_kernel_spmd(nc, [{f"in_{k}": a for k, a in arrays.items()}], core_ids=[0])
    return np.asarray(r.results[0]["out"]).reshape(N, D)
```
